# Optimizing a Trainium2 kernel written in Bass

```python
import numpy as np
import jax
import jax.numpy as jnp

def _softmax(x, axis=-1):
    return jax.nn.softmax(x, axis=axis)

def _gelu(x):
    return jax.nn.gelu(x, approximate=True)

def _silu(x):
    return jax.nn.silu(x)

def _sigmoid(x):
    return jax.nn.sigmoid(x)

def _layernorm(x, axis=-1, eps=1e-05):
    m = jnp.mean(x, axis=axis, keepdims=True)
    v = jnp.var(x, axis=axis, keepdims=True)
    return (x - m) / jnp.sqrt(v + eps)

def _scatter_add(tgt, idx, src, axis=0):
    return tgt.at[idx].add(src)

def _segment_sum(src, seg, n):
    return jax.ops.segment_sum(src, seg, n)
kernel_name = 'mk_seq_postln_d4_jaxref_r4_6b13e6'

def setup_inputs(seed: int=0):
    np.random.seed(seed)
    _w = jnp.asarray

    def _L0_attn_setup():
        import jax, jax.numpy as jnp
        import numpy as np
        B, N, D = (8, 256, 1024)
        H = 8
        HEAD_DIM = D // H
        E = HEAD_DIM // H
        key = jax.random.key(seed)
        ks = jax.random.split(key, 7)
        s = 0.02
        return {'x': jax.random.normal(ks[0], (B, N, D), dtype=jnp.float32), 'Wqk_w': jax.random.normal(ks[1], (2 * HEAD_DIM, D), dtype=jnp.float32) * s, 'Wqk_b': jnp.zeros((2 * HEAD_DIM,), dtype=jnp.float32), 'Wv_w': jax.random.normal(ks[2], (HEAD_DIM, D), dtype=jnp.float32) * s, 'Wv_b': jnp.zeros((HEAD_DIM,), dtype=jnp.float32), 'Wo_w': jax.random.normal(ks[3], (D, HEAD_DIM), dtype=jnp.float32) * s, 'Wo_b': jnp.zeros((D,), dtype=jnp.float32)}
    _L0_attn_in = _L0_attn_setup()

    def _L0_ffn_setup():
        import jax, jax.numpy as jnp
        import numpy as np
        B, L, H, Dh, M = (4, 512, 16, 64, 256)
        D = H * Dh
        key = jax.random.key(seed)
        kx, ku, kd, kp = jax.random.split(key, 4)
        x = jax.random.normal(kx, (B, L, D), dtype=jnp.float32)
        up = jax.random.normal(ku, (H, Dh, M), dtype=jnp.float32)
        down = jax.random.normal(kd, (H, M, Dh), dtype=jnp.float32)
        perm = jax.random.permutation(kp, D)
        return {'x': x, 'up': up, 'down': down, 'perm': perm}
    _L0_ffn_in = _L0_ffn_setup()

    def _L1_attn_setup():
        import jax, jax.numpy as jnp
        import numpy as np
        from jax import lax
        BLOCK_LEN = 128
        NEG_INF = -1000000000.0
        key = jax.random.key(seed)
        ks = jax.random.split(key, 8)
        N, L, Dm = (2, 2048, 1024)
        W, H, dh = (256, 16, 64)
        s = lambda fan: 1.0 / np.sqrt(fan)
        return {'inputs': jax.random.normal(ks[0], (N, L, Dm), jnp.float32), 'conv_w': jax.random.normal(ks[1], (3, Dm, 3 * W), jnp.float32) * s(3 * Dm), 'conv_b': jnp.zeros((3 * W,), jnp.float32), 'wq': jax.random.normal(ks[2], (W, H, dh), jnp.float32) * s(W), 'bq': jnp.zeros((H, dh), jnp.float32), 'wk': jax.random.normal(ks[3], (W, H, dh), jnp.float32) * s(W), 'bk': jnp.zeros((H, dh), jnp.float32), 'wv': jax.random.normal(ks[4], (W, H, dh), jnp.float32) * s(W), 'bv': jnp.zeros((H, dh), jnp.float32), 'wo': jax.random.normal(ks[5], (H, dh, W), jnp.float32) * s(H * dh), 'bo': jnp.zeros((W,), jnp.float32), 'proj_w': jax.random.normal(ks[6], (W, Dm), jnp.float32) * s(W), 'proj_b': jnp.zeros((Dm,), jnp.float32)}
    _L1_attn_in = _L1_attn_setup()

    def _L1_ffn_setup():
        import jax, jax.numpy as jnp
        import numpy as np

        @jax.custom_vjp
        def ste_sign(w):
            return jnp.sign(w)

        def _ste_fwd(w):
            return (jnp.sign(w), w)

        def _ste_bwd(w, g):
            mask = ((w > -1) & (w < 1)).astype(g.dtype)
            return (g * mask,)
        ste_sign.defvjp(_ste_fwd, _ste_bwd)
        key = jax.random.key(seed)
        k = jax.random.split(key, 6)
        B, S, H, O, E = (4, 512, 1024, 1024, 8)
        return {'x': jax.random.normal(k[0], (B, S, H), dtype=jnp.float32), 'weight': jax.random.normal(k[1], (O, H), dtype=jnp.float32) * 0.02, 'bias': jax.random.normal(k[2], (O,), dtype=jnp.float32) * 0.02, 'gate_w': jax.random.normal(k[3], (E, H), dtype=jnp.float32) * 0.02, 'in_channel_scale': jax.random.normal(k[4], (E, H), dtype=jnp.float32), 'out_channel_scale': jax.random.normal(k[5], (E, O), dtype=jnp.float32)}
    _L1_ffn_in = _L1_ffn_setup()

    def _L2_attn_setup():
        import jax, jax.numpy as jnp
        import numpy as np
        from jax import lax
        H = 1024
        DIN = 2048
        N = 16
        K = 4
        R = 64
        B_SZ = 2
        L = 512
        EPS = 1e-06

        def rmsnorm(x, w):
            return x * lax.rsqrt(jnp.mean(x * x, axis=-1, keepdims=True) + EPS) * w

        def _selective_scan(x, dt, A, Bm, Cm):
            xT = jnp.transpose(x, (2, 0, 1))
            dtT = jnp.transpose(dt, (2, 0, 1))
            BT = jnp.transpose(Bm, (2, 0, 1))
            CT = jnp.transpose(Cm, (2, 0, 1))

            def step(h, inp):
                x_t, dt_t, B_t, C_t = inp
                dA = jnp.exp(dt_t[..., None] * A)
                dBx = dt_t[..., None] * B_t[:, None, :] * x_t[..., None]
                h = dA * h + dBx
                y = jnp.einsum('bdn,bn->bd', h, C_t)
                return (h, y)
            h0 = jnp.zeros((x.shape[0], x.shape[1], A.shape[1]), dtype=x.dtype)
            _, ys = lax.scan(step, h0, (xT, dtT, BT, CT))
            return jnp.transpose(ys, (1, 2, 0))
        key = jax.random.key(seed)
        ks = jax.random.split(key, 8)
        hidden_states = jax.random.normal(ks[0], (B_SZ, L, H), dtype=jnp.float32)
        s = 0.02
        in_proj_w = jax.random.normal(ks[1], (H, 2 * DIN), dtype=jnp.float32) * s
        conv_w = jax.random.normal(ks[2], (DIN, K), dtype=jnp.float32) * 0.2
        conv_b = jax.random.normal(ks[3], (DIN,), dtype=jnp.float32) * 0.02
        x_proj_w = jax.random.normal(ks[4], (R + 2 * N, DIN), dtype=jnp.float32) * s
        dt_proj_w = jax.random.normal(ks[5], (DIN, R), dtype=jnp.float32) * s
        dt_bias = jax.random.normal(ks[6], (DIN,), dtype=jnp.float32) * 0.5 - 4.0
        A_log = jnp.log(jnp.broadcast_to(jnp.arange(1, N + 1, dtype=jnp.float32)[None, :], (DIN, N)))
        D_param = jnp.ones((DIN,), dtype=jnp.float32)
        out_proj_w = jax.random.normal(ks[7], (H, DIN), dtype=jnp.float32) * s
        dt_ln_w = jnp.ones((R,), dtype=jnp.float32)
        B_ln_w = jnp.ones((N,), dtype=jnp.float32)
        C_ln_w = jnp.ones((N,), dtype=jnp.float32)
        return dict(hidden_states=hidden_states, in_proj_w=in_proj_w, conv_w=conv_w, conv_b=conv_b, x_proj_w=x_proj_w, dt_proj_w=dt_proj_w, dt_bias=dt_bias, A_log=A_log, D_param=D_param, out_proj_w=out_proj_w, dt_ln_w=dt_ln_w, B_ln_w=B_ln_w, C_ln_w=C_ln_w)
    _L2_attn_in = _L2_attn_setup()

    def _L2_ffn_setup():
        import jax, jax.numpy as jnp
        import numpy as np
        IN_F = 1024
        OUT_F = 1024
        GS = 128

        def _dequantize_groupwise_int4(w_packed, w_scales):
            low = (w_packed & 15) - 8
            high = (w_packed >> 4 & 15) - 8
            q = jnp.stack([low, high], axis=-1).reshape(OUT_F, IN_F).astype(jnp.float32)
            w = q.reshape(OUT_F, IN_F // GS, GS) * w_scales[:, :, None]
            return w.reshape(OUT_F, IN_F)
        key = jax.random.key(seed)
        ks = jax.random.split(key, 5)
        x = jax.random.normal(ks[0], (4, 512, IN_F), dtype=jnp.float32)
        w_packed = jax.random.randint(ks[1], (OUT_F, IN_F // 2), 0, 64, dtype=jnp.int32)
        w_scales = jax.random.uniform(ks[2], (OUT_F, IN_F // GS), dtype=jnp.float32, minval=0.005, maxval=0.02)
        perm = jax.random.permutation(ks[3], IN_F).astype(jnp.int32)
        bias = jax.random.normal(ks[4], (OUT_F,), dtype=jnp.float32) * 0.01
        return {'x': x, 'w_packed': w_packed, 'w_scales': w_scales, 'perm': perm, 'bias': bias}
    _L2_ffn_in = _L2_ffn_setup()

    def _L3_attn_setup():
        import jax, jax.numpy as jnp
        import numpy as np
        H = 1024
        D = H // 4
        key = jax.random.key(seed)
        k1, k2, k3, k4, k5 = jax.random.split(key, 5)
        x = jax.random.normal(k1, (4, 1024, H), dtype=jnp.float32)
        s_in = 1.0 / np.sqrt(H)
        Wqkv = jax.random.normal(k2, (H, 3 * D), dtype=jnp.float32) * s_in
        bqkv = jax.random.normal(k3, (3 * D,), dtype=jnp.float32) * 0.01
        Wo = jax.random.normal(k4, (D, H), dtype=jnp.float32) * (1.0 / np.sqrt(D))
        bo = jax.random.normal(k5, (H,), dtype=jnp.float32) * 0.01
        return {'x': x, 'Wqkv': Wqkv, 'bqkv': bqkv, 'Wo': Wo, 'bo': bo}
    _L3_attn_in = _L3_attn_setup()

    def _L3_ffn_setup():
        import jax, jax.numpy as jnp
        import numpy as np
        SCALING = 32.0 / 16.0
        key = jax.random.key(seed)
        ks = jax.random.split(key, 7)
        B, T, D, O, R, E = (4, 512, 1024, 1024, 16, 8)
        x = jax.random.normal(ks[0], (B, T, D), dtype=jnp.float32)
        base_W = jax.random.normal(ks[1], (O, D), dtype=jnp.float32) * D ** (-0.5)
        base_b = jax.random.normal(ks[2], (O,), dtype=jnp.float32) * 0.01
        router_W = jax.random.normal(ks[3], (2 * E - 1, D), dtype=jnp.float32) * D ** (-0.5)
        router_b = jax.random.normal(ks[4], (2 * E - 1,), dtype=jnp.float32) * 0.01
        A = jax.random.normal(ks[5], (E, R, D), dtype=jnp.float32) * D ** (-0.5)
        Bm = jax.random.normal(ks[6], (E, O, R), dtype=jnp.float32) * R ** (-0.5)
        assigned_idx = 0
        others = [i for i in range(E) if i != assigned_idx]
        expert_map = jnp.array([assigned_idx] * E + others, dtype=jnp.int32)
        return {'x': x, 'base_W': base_W, 'base_b': base_b, 'router_W': router_W, 'router_b': router_b, 'A': A, 'B': Bm, 'expert_map': expert_map}
    _L3_ffn_in = _L3_ffn_setup()
    _d = {'L0_attn_x': _L0_attn_in['x'], 'L0_attn_Wqk_w': _L0_attn_in['Wqk_w'], 'L0_attn_Wqk_b': _L0_attn_in['Wqk_b'], 'L0_attn_Wv_w': _L0_attn_in['Wv_w'], 'L0_attn_Wv_b': _L0_attn_in['Wv_b'], 'L0_attn_Wo_w': _L0_attn_in['Wo_w'], 'L0_attn_Wo_b': _L0_attn_in['Wo_b'], 'L0_ffn_up': _L0_ffn_in['up'], 'L0_ffn_down': _L0_ffn_in['down'], 'L0_ffn_perm': _L0_ffn_in['perm'], 'L1_attn_conv_w': _L1_attn_in['conv_w'], 'L1_attn_conv_b': _L1_attn_in['conv_b'], 'L1_attn_wq': _L1_attn_in['wq'], 'L1_attn_bq': _L1_attn_in['bq'], 'L1_attn_wk': _L1_attn_in['wk'], 'L1_attn_bk': _L1_attn_in['bk'], 'L1_attn_wv': _L1_attn_in['wv'], 'L1_attn_bv': _L1_attn_in['bv'], 'L1_attn_wo': _L1_attn_in['wo'], 'L1_attn_bo': _L1_attn_in['bo'], 'L1_attn_proj_w': _L1_attn_in['proj_w'], 'L1_attn_proj_b': _L1_attn_in['proj_b'], 'L1_ffn_weight': _L1_ffn_in['weight'], 'L1_ffn_bias': _L1_ffn_in['bias'], 'L1_ffn_gate_w': _L1_ffn_in['gate_w'], 'L1_ffn_in_channel_scale': _L1_ffn_in['in_channel_scale'], 'L1_ffn_out_channel_scale': _L1_ffn_in['out_channel_scale'], 'L2_attn_in_proj_w': _L2_attn_in['in_proj_w'], 'L2_attn_conv_w': _L2_attn_in['conv_w'], 'L2_attn_conv_b': _L2_attn_in['conv_b'], 'L2_attn_x_proj_w': _L2_attn_in['x_proj_w'], 'L2_attn_dt_proj_w': _L2_attn_in['dt_proj_w'], 'L2_attn_dt_bias': _L2_attn_in['dt_bias'], 'L2_attn_A_log': _L2_attn_in['A_log'], 'L2_attn_D_param': _L2_attn_in['D_param'], 'L2_attn_out_proj_w': _L2_attn_in['out_proj_w'], 'L2_attn_dt_ln_w': _L2_attn_in['dt_ln_w'], 'L2_attn_B_ln_w': _L2_attn_in['B_ln_w'], 'L2_attn_C_ln_w': _L2_attn_in['C_ln_w'], 'L2_ffn_w_packed': _L2_ffn_in['w_packed'], 'L2_ffn_w_scales': _L2_ffn_in['w_scales'], 'L2_ffn_perm': _L2_ffn_in['perm'], 'L2_ffn_bias': _L2_ffn_in['bias'], 'L3_attn_Wqkv': _L3_attn_in['Wqkv'], 'L3_attn_bqkv': _L3_attn_in['bqkv'], 'L3_attn_Wo': _L3_attn_in['Wo'], 'L3_attn_bo': _L3_attn_in['bo'], 'L3_ffn_base_W': _L3_ffn_in['base_W'], 'L3_ffn_base_b': _L3_ffn_in['base_b'], 'L3_ffn_router_W': _L3_ffn_in['router_W'], 'L3_ffn_router_b': _L3_ffn_in['router_b'], 'L3_ffn_A': _L3_ffn_in['A'], 'L3_ffn_B': _L3_ffn_in['B'], 'L3_ffn_expert_map': _L3_ffn_in['expert_map']}
    _x0 = _d['L0_attn_x']
    _d['L0_attn_x'] = jax.random.normal(jax.random.fold_in(jax.random.key(seed), 1), (2, 1024, 1024), dtype=_x0.dtype)
    del _x0
    return _d

def reference(L0_attn_x, L0_attn_Wqk_w, L0_attn_Wqk_b, L0_attn_Wv_w, L0_attn_Wv_b, L0_attn_Wo_w, L0_attn_Wo_b, L0_ffn_up, L0_ffn_down, L0_ffn_perm, L1_attn_conv_w, L1_attn_conv_b, L1_attn_wq, L1_attn_bq, L1_attn_wk, L1_attn_bk, L1_attn_wv, L1_attn_bv, L1_attn_wo, L1_attn_bo, L1_attn_proj_w, L1_attn_proj_b, L1_ffn_weight, L1_ffn_bias, L1_ffn_gate_w, L1_ffn_in_channel_scale, L1_ffn_out_channel_scale, L2_attn_in_proj_w, L2_attn_conv_w, L2_attn_conv_b, L2_attn_x_proj_w, L2_attn_dt_proj_w, L2_attn_dt_bias, L2_attn_A_log, L2_attn_D_param, L2_attn_out_proj_w, L2_attn_dt_ln_w, L2_attn_B_ln_w, L2_attn_C_ln_w, L2_ffn_w_packed, L2_ffn_w_scales, L2_ffn_perm, L2_ffn_bias, L3_attn_Wqkv, L3_attn_bqkv, L3_attn_Wo, L3_attn_bo, L3_ffn_base_W, L3_ffn_base_b, L3_ffn_router_W, L3_ffn_router_b, L3_ffn_A, L3_ffn_B, L3_ffn_expert_map):

    def _L0_attn_ref(x, Wqk_w, Wqk_b, Wv_w, Wv_b, Wo_w, Wo_b):
        import jax, jax.numpy as jnp
        import numpy as np
        B, N, D = (8, 256, 1024)
        H = 8
        HEAD_DIM = D // H
        E = HEAD_DIM // H
        b, n, _ = x.shape
        qk = (x @ Wqk_w.T + Wqk_b).reshape(b, n, H, E, 2)
        q = jnp.transpose(qk[..., 0], (0, 2, 1, 3))
        k = jnp.transpose(qk[..., 1], (0, 2, 1, 3))
        v = (x @ Wv_w.T + Wv_b).reshape(b, n, H, E)
        v = jnp.transpose(v, (0, 2, 1, 3))
        scores = jnp.einsum('bhqd,bhkd->bhqk', q, k)
        attn = jax.nn.softmax(scores, axis=-1) / jnp.asarray(HEAD_DIM ** 0.5, x.dtype)
        out = jnp.einsum('bhsl,bhlv->bhsv', attn, v)
        out = jnp.transpose(out, (0, 2, 1, 3)).reshape(b, n, H * E)
        return out @ Wo_w.T + Wo_b

    def _L0_ffn_ref(x, up, down, perm):
        import jax, jax.numpy as jnp
        import numpy as np
        B, L, H, Dh, M = (4, 512, 16, 64, 256)
        D = H * Dh
        b, l, Dm = x.shape
        h, d = (up.shape[0], up.shape[1])
        unperm = jnp.argsort(perm)
        t = x.reshape(b * l, Dm)
        t = t[:, perm]
        t = t.reshape(b * l, h, d)
        t = jnp.einsum('bhd,hdm->bhm', t, up)
        t = jax.nn.gelu(t, approximate=False)
        t = jnp.einsum('bhm,hmd->bhd', t, down)
        t = t.reshape(b * l, h * d)
        t = t[:, unperm]
        out = t.reshape(b, l, Dm)
        return out

    def _L1_attn_ref(inputs, conv_w, conv_b, wq, bq, wk, bk, wv, bv, wo, bo, proj_w, proj_b):
        import jax, jax.numpy as jnp
        import numpy as np
        from jax import lax
        BLOCK_LEN = 128
        NEG_INF = -1000000000.0
        N, L, Dm = inputs.shape
        x = lax.conv_general_dilated(inputs, conv_w, window_strides=(1,), padding='SAME', dimension_numbers=('NWC', 'WIO', 'NWC')) + conv_b
        q, k, v = jnp.split(x, 3, axis=-1)
        W_ = q.shape[-1]
        nb = L // BLOCK_LEN
        q = q.reshape(N * nb, BLOCK_LEN, W_)
        k = k.reshape(N * nb, BLOCK_LEN, W_)
        v = v.reshape(N * nb, BLOCK_LEN, W_)
        dh = wq.shape[-1]
        qh = jnp.einsum('btd,dhe->bthe', q, wq) + bq
        kh = jnp.einsum('btd,dhe->bthe', k, wk) + bk
        vh = jnp.einsum('btd,dhe->bthe', v, wv) + bv
        scale = 1.0 / jnp.sqrt(jnp.asarray(dh, qh.dtype))
        scores = jnp.einsum('bqhe,bkhe->bhqk', qh * scale, kh)
        causal = jnp.tril(jnp.ones((BLOCK_LEN, BLOCK_LEN), bool))
        scores = jnp.where(causal, scores, NEG_INF)
        p = jax.nn.softmax(scores, axis=-1)
        o = jnp.einsum('bhqk,bkhe->bqhe', p, vh)
        o = jnp.einsum('bqhe,hed->bqd', o, wo) + bo
        o = o.reshape(N, L, W_)
        return o @ proj_w + proj_b

    def _L1_ffn_ref(x, weight, bias, gate_w, in_channel_scale, out_channel_scale):
        import jax, jax.numpy as jnp
        import numpy as np

        @jax.custom_vjp
        def ste_sign(w):
            return jnp.sign(w)

        def _ste_fwd(w):
            return (jnp.sign(w), w)

        def _ste_bwd(w, g):
            mask = ((w > -1) & (w < 1)).astype(g.dtype)
            return (g * mask,)
        ste_sign.defvjp(_ste_fwd, _ste_bwd)
        B, S, H = x.shape
        xf = x.reshape(-1, H)
        router_logits = xf @ gate_w.T
        routing = jax.nn.softmax(router_logits.astype(jnp.float32), axis=1).astype(x.dtype)
        in_scale = routing @ in_channel_scale
        out_scale = routing @ out_channel_scale
        wb = ste_sign(weight)
        out = xf * in_scale @ wb.T * out_scale + bias
        return out.reshape(B, S, -1)

    def _L2_attn_ref(hidden_states, in_proj_w, conv_w, conv_b, x_proj_w, dt_proj_w, dt_bias, A_log, D_param, out_proj_w, dt_ln_w, B_ln_w, C_ln_w):
        import jax, jax.numpy as jnp
        import numpy as np
        from jax import lax
        H = 1024
        DIN = 2048
        N = 16
        K = 4
        R = 64
        B_SZ = 2
        L = 512
        EPS = 1e-06

        def rmsnorm(x, w):
            return x * lax.rsqrt(jnp.mean(x * x, axis=-1, keepdims=True) + EPS) * w

        def _selective_scan(x, dt, A, Bm, Cm):
            xT = jnp.transpose(x, (2, 0, 1))
            dtT = jnp.transpose(dt, (2, 0, 1))
            BT = jnp.transpose(Bm, (2, 0, 1))
            CT = jnp.transpose(Cm, (2, 0, 1))

            def step(h, inp):
                x_t, dt_t, B_t, C_t = inp
                dA = jnp.exp(dt_t[..., None] * A)
                dBx = dt_t[..., None] * B_t[:, None, :] * x_t[..., None]
                h = dA * h + dBx
                y = jnp.einsum('bdn,bn->bd', h, C_t)
                return (h, y)
            h0 = jnp.zeros((x.shape[0], x.shape[1], A.shape[1]), dtype=x.dtype)
            _, ys = lax.scan(step, h0, (xT, dtT, BT, CT))
            return jnp.transpose(ys, (1, 2, 0))
        proj = hidden_states @ in_proj_w
        x, z = jnp.split(proj, 2, axis=-1)
        x = jnp.transpose(x, (0, 2, 1))
        z = jnp.transpose(z, (0, 2, 1))
        Lq = x.shape[-1]
        xp = jnp.pad(x, ((0, 0), (0, 0), (K - 1, 0)))
        xc = conv_b[None, :, None]
        for k in range(K):
            xc = xc + conv_w[None, :, k:k + 1] * xp[:, :, k:k + Lq]
        xc = jax.nn.silu(xc)
        ssm_p = jnp.einsum('bdl,ed->ble', xc, x_proj_w)
        dt_r = rmsnorm(ssm_p[..., :R], dt_ln_w)
        Bm = rmsnorm(ssm_p[..., R:R + N], B_ln_w)
        Cm = rmsnorm(ssm_p[..., R + N:], C_ln_w)
        dt = jnp.einsum('blr,dr->bdl', dt_r, dt_proj_w)
        dt = jax.nn.softplus(dt + dt_bias[None, :, None])
        A = -jnp.exp(A_log)
        Bm = jnp.transpose(Bm, (0, 2, 1))
        Cm = jnp.transpose(Cm, (0, 2, 1))
        ys = _selective_scan(xc, dt, A, Bm, Cm)
        y = (ys + D_param[None, :, None] * xc) * jax.nn.silu(z)
        return jnp.einsum('bdl,hd->blh', y, out_proj_w)

    def _L2_ffn_ref(x, w_packed, w_scales, perm, bias):
        import jax, jax.numpy as jnp
        import numpy as np
        IN_F = 1024
        OUT_F = 1024
        GS = 128

        def _dequantize_groupwise_int4(w_packed, w_scales):
            low = (w_packed & 15) - 8
            high = (w_packed >> 4 & 15) - 8
            q = jnp.stack([low, high], axis=-1).reshape(OUT_F, IN_F).astype(jnp.float32)
            w = q.reshape(OUT_F, IN_F // GS, GS) * w_scales[:, :, None]
            return w.reshape(OUT_F, IN_F)
        shape = x.shape
        xf = x.reshape(-1, IN_F)[:, perm]
        w = _dequantize_groupwise_int4(w_packed, w_scales)
        y = xf @ w.T
        return y.reshape(*shape[:-1], OUT_F) + bias

    def _L3_attn_ref(x, Wqkv, bqkv, Wo, bo):
        import jax, jax.numpy as jnp
        import numpy as np
        H = 1024
        D = H // 4
        B, S, C = x.shape
        d = C // 4
        qkv = jnp.einsum('bsc,cf->bsf', x, Wqkv) + bqkv
        qkv = qkv.reshape(B, S, 3, d)
        q, k, v = (qkv[:, :, 0], qkv[:, :, 1], qkv[:, :, 2])
        scale = 1.0 / jnp.sqrt(jnp.float32(d)).astype(x.dtype)
        attn = jnp.einsum('bqd,bkd->bqk', q, k) * scale
        attn = jax.nn.softmax(attn, axis=-1)
        out = jnp.einsum('bqk,bkd->bqd', attn, v)
        return jnp.einsum('bqd,dc->bqc', out, Wo) + bo

    def _L3_ffn_ref(x, base_W, base_b, router_W, router_b, A, B, expert_map):
        import jax, jax.numpy as jnp
        import numpy as np
        SCALING = 32.0 / 16.0
        E = A.shape[0]
        base_out = jnp.einsum('btd,od->bto', x, base_W) + base_b
        logits = jnp.einsum('btd,nd->btn', x, router_W) + router_b
        probs = jax.nn.softmax(logits, axis=-1)
        topk_p, topk_i = jax.lax.top_k(probs, E)
        mapped = expert_map[topk_i]
        onehot = (mapped[..., None] == jnp.arange(E)).astype(x.dtype)
        w = jnp.einsum('btk,btke->bte', topk_p, onehot)
        h = jnp.einsum('btd,erd->bter', x, A)
        lora = jnp.einsum('bter,eor->bto', h * w[..., None], B) * SCALING
        return base_out + lora
    x = L0_attn_x
    x = _layernorm(x + _L0_attn_ref(x, L0_attn_Wqk_w, L0_attn_Wqk_b, L0_attn_Wv_w, L0_attn_Wv_b, L0_attn_Wo_w, L0_attn_Wo_b), axis=-1)
    x = _layernorm(x + _L0_ffn_ref(x, L0_ffn_up, L0_ffn_down, L0_ffn_perm), axis=-1)
    x = _layernorm(x + _L1_attn_ref(x, L1_attn_conv_w, L1_attn_conv_b, L1_attn_wq, L1_attn_bq, L1_attn_wk, L1_attn_bk, L1_attn_wv, L1_attn_bv, L1_attn_wo, L1_attn_bo, L1_attn_proj_w, L1_attn_proj_b), axis=-1)
    x = _layernorm(x + _L1_ffn_ref(x, L1_ffn_weight, L1_ffn_bias, L1_ffn_gate_w, L1_ffn_in_channel_scale, L1_ffn_out_channel_scale), axis=-1)
    x = _layernorm(x + _L2_attn_ref(x, L2_attn_in_proj_w, L2_attn_conv_w, L2_attn_conv_b, L2_attn_x_proj_w, L2_attn_dt_proj_w, L2_attn_dt_bias, L2_attn_A_log, L2_attn_D_param, L2_attn_out_proj_w, L2_attn_dt_ln_w, L2_attn_B_ln_w, L2_attn_C_ln_w), axis=-1)
    x = _layernorm(x + _L2_ffn_ref(x, L2_ffn_w_packed, L2_ffn_w_scales, L2_ffn_perm, L2_ffn_bias), axis=-1)
    x = _layernorm(x + _L3_attn_ref(x, L3_attn_Wqkv, L3_attn_bqkv, L3_attn_Wo, L3_attn_bo), axis=-1)
    x = _layernorm(x + _L3_ffn_ref(x, L3_ffn_base_W, L3_ffn_base_b, L3_ffn_router_W, L3_ffn_router_b, L3_ffn_A, L3_ffn_B, L3_ffn_expert_map), axis=-1)
    return x

_drawn_inputs = setup_inputs


def setup_inputs(seed=0):
    import zlib

    import numpy as np

    out = dict(_drawn_inputs(seed))
    spreads = {'L0_attn_Wqk_b': (0.0, 0.8),
     'L0_attn_Wv_b': (0.0, 0.8),
     'L0_attn_Wo_b': (0.0, 0.1),
     'L1_attn_conv_b': (0.0, 0.1),
     'L1_attn_bq': (0.0, 0.435),
     'L1_attn_bk': (0.0, 0.8),
     'L1_attn_bv': (0.0, 0.1),
     'L1_attn_bo': (0.0, 0.1),
     'L1_attn_proj_b': (0.0, 0.1),
     'L2_attn_D_param': (1.0, 0.6),
     'L2_attn_dt_ln_w': (1.0, 0.6),
     'L2_attn_B_ln_w': (1.0, 0.6),
     'L2_attn_C_ln_w': (1.0, 0.6)}
    factors = {'L0_attn_Wqk_w': 6.771,
     'L0_attn_Wv_w': 4.755,
     'L0_attn_Wo_w': 4.763,
     'L1_ffn_bias': 7.081,
     'L2_attn_conv_b': 8.0,
     'L2_attn_dt_proj_w': 8.0,
     'L2_attn_dt_bias': 8.0,
     'L2_attn_A_log': 5.676,
     'L2_ffn_bias': 6.515,
     'L3_attn_bqkv': 3.74,
     'L3_attn_bo': 5.281,
     'L3_ffn_base_b': 8.0,
     'L3_ffn_router_b': 7.326}
    for name, (base, spread) in spreads.items():
        noise = np.random.default_rng([zlib.crc32(name.encode()), seed]).standard_normal(out[name].shape)
        drawn = base * np.exp(spread * noise) if base else spread * noise
        out[name] = jnp.asarray(drawn.astype(out[name].dtype))
    for name, factor in factors.items():
        out[name] = (out[name] * factor).astype(out[name].dtype)
    return out
```

```python
import numpy as np
import concourse.bass as bass
from concourse import mybir
from contextlib import ExitStack

F32 = mybir.dt.float32
F32R = mybir.dt.float32r
I32 = mybir.dt.int32
U32 = mybir.dt.uint32
ACT = mybir.ActivationFunctionType
ALU = mybir.AluOpType
AX = mybir.AxisListType

P = 128
D = 1024
KT = D // P
BATCH, SEQ = 2, 1024
T = BATCH * SEQ
NT = 512
CHUNKS = T // NT
PAD = 1


def cols(X, c, shift=0):
    per = SEQ // NT
    at = PAD + (c % per) * NT + shift
    return X[:, :, c // per, at:at + NT]


class Stage:
    used = []

    def __init__(self, nc, name):
        self.nc, self.name, self.ctx, self.sems = nc, name, ExitStack(), []

    def __enter__(self):
        self.ctx.__enter__()
        return self

    def __exit__(self, *a):
        Stage.used += self.sems
        return self.ctx.__exit__(*a)

    def sb(self, name, shape, dt=F32):
        return self.ctx.enter_context(self.nc.sbuf_tensor(f"{self.name}_{name}", shape, dt))

    def ps(self, name, shape):
        return self.ctx.enter_context(self.nc.psum_tensor(f"{self.name}_{name}", shape, F32))

    def sem(self, name):
        self.sems.append(self.nc.alloc_semaphore(f"{self.name}_{name}"))
        return self.sems[-1]


def recycle(nc):
    nc.clear_and_free_semaphores(Stage.used)
    Stage.used = []
    nc.all_engine_barrier()


class Chain:

    def __init__(self, eng, sem):
        self.eng, self.sem, self.n = eng, sem, 0

    def link(self, ins):
        self.n += 1
        ins.then_inc(self.sem, 1)
        self.eng.wait_ge(self.sem, self.n)


class LayerNorm:

    def __init__(self, s, K):
        self.s, self.K = s, K
        self.z = s.sb("z", [P, 2, KT, NT])
        self.sq = s.sb("sq", [P, KT, NT])
        self.sum1 = s.sb("sum1", [P, 2, NT])
        self.sum2 = s.sb("sum2", [P, 2, NT])
        self.std = s.sb("std", [P, NT])
        self.rstd = s.sb("rstd", [P, NT])
        self.stats = s.ps("stats", [P, 2, NT])
        self.summed = s.sem("ln_summed")
        self.mean = s.sem("ln_mean")
        self.centred = s.sem("ln_centred")
        self.squared = s.sem("ln_squared")
        self.sqsummed = s.sem("ln_sqsummed")
        self.var = s.sem("ln_var")
        self.stdok = s.sem("ln_std")
        self.done = s.sem("ln_done")

    def v_sum(self, v, i, link):
        z = self.z[:, i % 2]
        v.tensor_reduce(self.sum1[:, i % 2], z.rearrange("p k t -> p t k"), AX.X, ALU.add).then_inc(self.summed, 1)

    def v_centre(self, v, i, link):
        z = self.z[:, i % 2]
        v.wait_ge(self.mean, i + 1)
        m = self.stats[:, 0:1, :].to_broadcast([P, KT, NT])
        v.tensor_tensor(z, z, m, ALU.subtract).then_inc(self.centred, 1)

    def v_sumsq(self, v, i, link):
        v.wait_ge(self.squared, i + 1)
        v.tensor_reduce(self.sum2[:, i % 2], self.sq.rearrange("p k t -> p t k"), AX.X, ALU.add).then_inc(self.sqsummed, 1)

    def v_scale(self, v, i, link, out):
        v.wait_ge(self.stdok, i + 1)
        link(v.reciprocal(self.rstd[:, :], self.std[:, :]))
        z = self.z[:, i % 2]
        r = self.rstd[:, None, :].to_broadcast([P, KT, NT])
        v.tensor_tensor(out, z, r, ALU.mult).then_inc(self.done, 1)

    def t_mean(self, t, i):
        t.wait_ge(self.summed, i + 1)
        if i:
            t.wait_ge(self.centred, i)
        t.matmul(self.stats[:, 0, :], self.K.mean_w[:, :], self.sum1[:, i % 2], start=True, stop=True).then_inc(self.mean, 1)

    def t_var(self, t, i):
        t.wait_ge(self.sqsummed, i + 1)
        if i:
            t.wait_ge(self.stdok, i)
        t.matmul(self.stats[:, 1, :], self.K.mean_w[:, :], self.sum2[:, i % 2], start=True, stop=True).then_inc(self.var, 1)

    def a_square(self, a, i):
        a.wait_ge(self.centred, i + 1)
        if i:
            a.wait_ge(self.sqsummed, i)
        a.activation(self.sq[:, :, :], self.z[:, i % 2], ACT.Square).then_inc(self.squared, 1)

    def a_std(self, a, i):
        a.wait_ge(self.var, i + 1)
        if i:
            a.wait_ge(self.done, i)
        a.activation(self.std[:, :], self.stats[:, 1, :], ACT.Sqrt, bias=self.K.eps[:, :]).then_inc(self.stdok, 1)


class Consts:

    def __init__(self, nc, ctx):
        sb = lambda n, s: ctx.enter_context(nc.sbuf_tensor(n, s, F32))
        self.X = sb("state", [P, KT, BATCH, PAD + SEQ + PAD])
        self.mean_w = sb("mean_w", [P, P])
        self.eps = sb("eps", [P, 1])
        self.eps6 = sb("eps6", [P, 1])
        self.ident = sb("ident", [P, P])
        self.one = sb("one", [P, 1])
        self.out_stored = ctx.enter_context(nc.semaphore("out_stored"))
        with nc.semaphore("const_set") as set_, nc.Block() as block:
            @block.vector
            def _(v):
                v.memset(self.mean_w[:, :], 1.0 / D)
                v.memset(self.eps[:, :], 1e-5)
                v.memset(self.eps6[:, :], 1e-6)
                v.memset(self.one[:, :], 1.0)
                for b in range(BATCH):
                    v.memset(self.X[:, :, b, 0:PAD], 0.0)
                    v.memset(self.X[:, :, b, PAD + SEQ:], 0.0)

            @block.gpsimd
            def _(g):
                g.memset(self.ident[:, :], 0.0).then_inc(set_, 1)
                g.wait_ge(set_, 1)
                g.affine_select(out=self.ident[:, :], in_=self.ident[:, :], compare_op=ALU.not_equal,
                                fill=1.0, base=0, pattern=[[-1, P]], channel_multiplier=1)


ACC = 4


class DenseLN:

    MEAN_AT, VAR_AT = 0, 5
    CENTRE_AT, SUMSQ_AT, SCALE_AT = 0, 3, 6

    def __init__(self, s, K, acc=ACC):
        self.s, self.K, self.ln, self.ACC = s, K, LayerNorm(s, K), acc
        self.acc = s.ps("acc", [P, acc, NT])
        self.acc_ready = s.sem("acc_ready")
        self.acc_free = s.sem("acc_free")
        self.v_order = s.sem("v_order")

    def t_before(self, t, i): pass
    def v_before(self, v, i): pass
    def a_before(self, a, i): pass
    def t_after(self, t, i, m): pass
    def v_after(self, v, i, m): pass
    def a_after(self, a, i): pass
    def t_start(self, t): pass
    def v_start(self, v): pass
    def a_start(self, a): pass

    def tensor(self, t):
        self.t_start(t)
        for i in range(CHUNKS):
            self.t_before(t, i)
            for m in range(KT):
                n = i * KT + m
                if n >= self.ACC:
                    t.wait_ge(self.acc_free, n - self.ACC + 1)
                self.t_tile(t, i, m, self.acc[:, n % self.ACC, :]).then_inc(self.acc_ready, 1)
                if i and m == self.MEAN_AT:
                    self.ln.t_mean(t, i - 1)
                if i and m == self.VAR_AT:
                    self.ln.t_var(t, i - 1)
                self.t_after(t, i, m)
        self.ln.t_mean(t, CHUNKS - 1)
        self.ln.t_var(t, CHUNKS - 1)

    def vector(self, v):
        link = Chain(v, self.v_order).link
        self.link = link
        self.v_start(v)
        for i in range(CHUNKS):
            self.v_before(v, i)
            if i >= 2:
                v.wait_ge(self.ln.done, i - 1)
            for m in range(KT):
                n = i * KT + m
                v.wait_ge(self.acc_ready, n + 1)
                self.v_tile(v, i, m, self.acc[:, n % self.ACC, :], self.ln.z[:, i % 2, m, :],
                            cols(self.K.X, i)[:, m, :]).then_inc(self.acc_free, 1)
                if i and m == self.CENTRE_AT:
                    self.ln.v_centre(v, i - 1, link)
                if i and m == self.SUMSQ_AT:
                    self.ln.v_sumsq(v, i - 1, link)
                if i and m == self.SCALE_AT:
                    self.ln.v_scale(v, i - 1, link, cols(self.K.X, i - 1))
                self.v_after(v, i, m)
            v.wait_ge(self.acc_free, (i + 1) * KT)
            self.ln.v_sum(v, i, link)
        self.ln.v_centre(v, CHUNKS - 1, link)
        self.ln.v_sumsq(v, CHUNKS - 1, link)
        self.ln.v_scale(v, CHUNKS - 1, link, cols(self.K.X, CHUNKS - 1))

    def gpsimd(self, g): pass

    def run(self, nc):
        with nc.Block() as block:
            @block.sync
            def _(e):
                self.sync(e)

            @block.gpsimd
            def _(g):
                self.gpsimd(g)

            @block.tensor
            def _(t):
                self.tensor(t)

            @block.vector
            def _(v):
                self.vector(v)

            @block.scalar
            def _(a):
                self.scalar(a)

    def scalar(self, a):
        self.a_start(a)
        for i in range(CHUNKS):
            self.a_before(a, i)
            if i:
                self.ln.a_square(a, i - 1)
                self.ln.a_std(a, i - 1)
            self.a_after(a, i)
        self.ln.a_square(a, CHUNKS - 1)
        self.ln.a_std(a, CHUNKS - 1)



HEADS, HE = 8, 16
HD = HEADS * HE
HP = 32
G = 4
GROUPS = HEADS // G
KTS = SEQ // P
SCALE = 1.0 / float(np.sqrt(HD))


class L0Attn:

    def __init__(self, nc, K, w):
        self.nc, self.K, self.w = nc, K, w

    def project(self, s, o):
        nc, K, w = self.nc, self.K, self.w
        W = s.sb("W", [P, KT, 3 * HD])
        idx = s.sb("idx", [P, KT], I32)
        idx2 = s.sb("idx2", [P, KT, BATCH], I32)
        b = s.sb("b", [P, 2])
        acc = s.ps("acc", [P, 4, NT])
        vacc = s.ps("vacc", [P, 2, NT])
        idx_in, b_in = s.sem("idx_in"), s.sem("b_in")
        idx2_ok = s.sem("idx2_ok")
        w_in = [s.sem(f"w_in{k}") for k in range(KT)]
        x_in = [[s.sem(f"x_in{k}_{b_}") for b_ in range(BATCH)] for k in range(KT)]
        acc_ready, hi_ok, lo_ok = s.sem("acc_ready"), s.sem("hi_ok"), s.sem("lo_ok")
        v_ready, v_ok = s.sem("v_ready"), s.sem("v_ok")
        with nc.Block() as block:
            @block.sync
            def _(e):
                e.dma_start(idx[:, :], w["perm"]).then_inc(idx_in, 16)
                e.dma_start(b[:, :], w["qk_b"]).then_inc(b_in, 16)

            @block.gpsimd
            def _(g):
                g.wait_ge(idx_in, 16)
                g.wait_ge(idx2_ok, BATCH)
                for b_ in range(BATCH):
                    for k in range(KT):
                        if b_ == 0:
                            g.indirect_dma_start(out=W[:, k, :], out_offset=None, in_=w["qkv_T"],
                                                 in_offset=bass.IndirectOffsetOnAxis(ap=idx[:, k:k + 1].bitcast(U32), axis=0)).then_inc(w_in[k], 16)
                        g.indirect_dma_start(out=K.X[:, k, b_, PAD:PAD + SEQ], out_offset=None, in_=w["x_rows"],
                                             in_offset=bass.IndirectOffsetOnAxis(ap=idx2[:, k, b_:b_ + 1].bitcast(U32), axis=0)).then_inc(x_in[k][b_], 16)

            @block.vector
            def _(v):
                v.wait_ge(idx_in, 16)
                for b_ in range(BATCH):
                    v.tensor_scalar(idx2[:, :, b_], idx[:, :], float(BATCH), float(b_), ALU.mult, ALU.add).then_inc(idx2_ok, 1)
                v.memset(o.v[:, :, :, HE:HP], 0.0).then_inc(idx2_ok, 1)
                v.wait_ge(idx2_ok, BATCH + 1)
                v.memset(o.v[:, :, :, HE:HE + 1], 1.0)
                v.wait_ge(b_in, 16)
                for i in range(CHUNKS):
                    for a_ in range(2):
                        n = 2 * i + a_
                        v.wait_ge(hi_ok, n + 1)
                        v.scalar_tensor_tensor(o.lo[:, a_, i * NT:(i + 1) * NT], acc[:, n % 4, :], b[:, a_:a_ + 1],
                                               o.hi[:, a_, i * NT:(i + 1) * NT].bitcast(F32), ALU.add, ALU.subtract).then_inc(lo_ok, 1)

            @block.scalar
            def _(a):
                a.wait_ge(b_in, 16)
                for i in range(CHUNKS):
                    for a_ in range(2):
                        n = 2 * i + a_
                        a.wait_ge(acc_ready, n + 1)
                        a.activation(o.hi[:, a_, i * NT:(i + 1) * NT], acc[:, n % 4, :], ACT.Identity, bias=b[:, a_:a_ + 1]).then_inc(hi_ok, 1)
                    for q in range(NT // P):
                        n = i * (NT // P) + q
                        a.wait_ge(v_ready, n + 1)
                        a.activation(o.v[:, n, :, 0:HE], vacc[:, n % 2, 0:HD].rearrange("p (h e) -> p h e", e=HE), ACT.Copy).then_inc(v_ok, 1)

            @block.tensor
            def _(t):
                for i in range(CHUNKS):
                    x = cols(K.X, i)
                    for a_ in range(2):
                        n = 2 * i + a_
                        if n >= 4:
                            t.wait_ge(lo_ok, n - 3)
                        for k in range(KT):
                            if n == 0:
                                t.wait_ge(w_in[k], 16)
                            if a_ == 0 and i % 2 == 0:
                                t.wait_ge(x_in[k][i // 2], 16)
                            last = t.matmul(acc[:, n % 4, :], W[:, k, a_ * HD:(a_ + 1) * HD], x[:, k, :], start=k == 0, stop=k == KT - 1)
                        last.then_inc(acc_ready, 1)
                    for q in range(NT // P):
                        n = i * (NT // P) + q
                        if n >= 2:
                            t.wait_ge(v_ok, n - 1)
                        for k in range(KT):
                            last = t.matmul(vacc[:, n % 2, 0:HD], x[:, k, q * P:(q + 1) * P], W[:, k, 2 * HD:], start=k == 0, stop=k == KT - 1)
                        last.then_inc(v_ready, 1)

    def attend(self, s, o):
        nc, K, w = self.nc, self.K, self.w
        sel = s.sb("sel", [P, 4, HEADS, P], F32R)
        onerow = s.sb("onerow", [P, 1])
        sumsel = s.sb("sumsel", [P, P])
        negm = s.sb("negm", [P, KTS])
        negh = s.sb("negh", [P, KTS], F32R)
        Q = s.sb("Q", [P, G, SEQ], F32R)
        Kk = s.sb("K", [P, G, SEQ], F32R)
        RING = 7
        PT = s.sb("PT", [P, RING, SEQ])
        selz = PT[:, 0:4, :].rearrange("p w (h c) -> p w h c", h=HEADS)
        mz = PT[:, 4, :].rearrange("p (q c) -> p q c", q=KTS)
        osb, rinv = PT[:, 5, :], PT[:, 6, :]
        bv = s.sb("bv", [P, GROUPS])
        bvs = s.sb("bvs", [P, GROUPS])
        S = s.ps("S", [P, 2, SEQ])
        st = s.ps("st", [P, 2, NT])
        O = s.ps("O", [P, SEQ])
        selz_ok, sel_ok, bv_in = s.sem("selz_ok"), s.sem("sel_ok"), s.sem("bv_in")
        stacked = s.sem("stacked")
        q_ok, k_ok = s.sem("q_ok"), s.sem("k_ok")
        s1, max_ok = s.sem("s1"), s.sem("max_ok")
        mz_ok, mT, qm_ok = s.sem("mz_ok"), s.sem("mT"), s.sem("qm_ok")
        s2, exp_ok, pv = s.sem("s2"), s.sem("exp_ok"), s.sem("pv")
        osb_ok, bsum, rinv_ok, o_ok, oT_ok = (s.sem(x) for x in ("osb_ok", "bsum", "rinv_ok", "o_ok", "oT_ok"))
        order = s.sem("order")
        steps = [(b, g) for b in range(BATCH) for g in range(GROUPS)]
        NST = 2 * G
        with nc.Block() as block:
            @block.sync
            def _(e):
                e.dma_start(bv[:, :], w["v_b"]).then_inc(bv_in, 16)

            @block.gpsimd
            def _(g):
                g.memset(selz[:, :, :, :], 0.0).then_inc(selz_ok, 1)
                g.memset(onerow[:, :], 0.0).then_inc(selz_ok, 1)
                g.memset(sumsel[:, :], 0.0).then_inc(selz_ok, 1)
                g.wait_ge(selz_ok, 3)
                for which, blks in enumerate(((0, 1), (2, 3), (0, 2), (1, 3))):
                    for blk in blks:
                        v = selz[:, which, :, blk * HP:blk * HP + HE]
                        g.affine_select(out=v, in_=v, compare_op=ALU.not_equal, fill=1.0, base=0,
                                        pattern=[[-HE, HEADS], [-1, HE]], channel_multiplier=1).then_inc(selz_ok, 1)
                for blk in (0, 2):
                    g.affine_select(out=onerow[:, :], in_=onerow[:, :], compare_op=ALU.not_equal, fill=1.0,
                                    base=-(blk * HP + HE), pattern=[[0, 1]], channel_multiplier=1).then_inc(selz_ok, 1)
                    g.wait_ge(selz_ok, 3 + 8 + blk // 2 + 1)
                v = sumsel[:, :].rearrange("p (j r) -> p j r", r=HP)
                g.affine_select(out=v, in_=v, compare_op=ALU.not_equal, fill=1.0, base=-HE,
                                pattern=[[-HP, G], [0, HP]], channel_multiplier=1).then_inc(selz_ok, 1)

            @block.vector
            def _(v):
                link = Chain(v, order).link
                v.wait_ge(selz_ok, 14)
                v.tensor_copy(sel[:, :, :, :], selz[:, :, :, :]).then_inc(sel_ok, 1)
                v.wait_ge(bv_in, 16)
                v.tensor_scalar(bvs[:, :], bv[:, :], SCALE, None, ALU.mult).then_inc(sel_ok, 1)
                for n, (b, g) in enumerate(steps):
                    for c in range(NST):
                        v.wait_ge(stacked, n * 2 * NST + 2 * c + 1)
                        v.tensor_copy(Q[:, c // 2, (c % 2) * NT:(c % 2 + 1) * NT], st[:, 0, :]).then_inc(q_ok, 1)
                    link(v.memset(mz, 0.0))
                    for h in range(G):
                        for qt in range(KTS):
                            m = (n * G + h) * KTS + qt
                            v.wait_ge(s1, m + 1)
                            if qt == 0 and n + h:
                                v.wait_ge(mz_ok, 2 * (n * G + h))
                            v.tensor_reduce(negm[:, qt:qt + 1], S[:, m % 2, :], AX.X, ALU.max, negate=True).then_inc(max_ok, 1)
                        m = n * G + h
                        v.wait_ge(max_ok, (m + 1) * KTS)
                        link(v.tensor_copy(negh[:, :], negm[:, :]))
                        if m:
                            v.wait_ge(mT, 2 * m)
                        v.tensor_copy(mz[:, :, HE], negh[:, :].bitcast(F32)).then_inc(mz_ok, 1)
                        v.tensor_tensor(mz[:, :, 2 * HP + HE], negm[:, :], negh[:, :].bitcast(F32), ALU.subtract).then_inc(mz_ok, 1)
                        for c in range(2):
                            v.wait_ge(mT, 2 * m + c + 1)
                            q = Q[:, h, c * NT:(c + 1) * NT]
                            v.tensor_tensor(q, q.bitcast(F32), st[:, c, :], ALU.add).then_inc(qm_ok, 1)
                    v.wait_ge(pv, (n + 1) * KTS)
                    if n:
                        v.wait_ge(o_ok, n)
                    v.tensor_copy(osb[:, :], O[:, :]).then_inc(osb_ok, 1)
                    v.wait_ge(bsum, n + 1)
                    link(v.reciprocal(rinv[:, :], S[:, 0, :]))
                    if n:
                        v.wait_ge(oT_ok, n)
                    v.tensor_tensor(osb[:, :], osb[:, :], rinv[:, :], ALU.mult).then_inc(o_ok, 1)

            @block.scalar
            def _(a):
                a.wait_ge(selz_ok, 14)
                a.wait_ge(sel_ok, 2)
                for n, (b, g) in enumerate(steps):
                    if n:
                        a.wait_ge(oT_ok, n)
                    for c in range(NST):
                        a.wait_ge(stacked, n * 2 * NST + 2 * c + 2)
                        a.activation(Kk[:, c // 2, (c % 2) * NT:(c % 2 + 1) * NT], st[:, 1, :], ACT.Identity, bias=onerow[:, :]).then_inc(k_ok, 1)
                    for kt in range(KTS):
                        for h in range(G):
                            m = (n * KTS + kt) * G + h
                            j = kt * G + h
                            if j >= RING:
                                a.wait_ge(pv, n * KTS + (j - RING) // G + 1)
                            a.wait_ge(s2, m + 1)
                            a.activation(PT[:, j % RING, :], S[:, m % 2, :], ACT.Exp).then_inc(exp_ok, 1)
                    a.wait_ge(o_ok, n + 1)
                    a.activation(o.oT[:, g, b * SEQ:(b + 1) * SEQ], osb[:, :], ACT.Identity, scale=SCALE, bias=bvs[:, g:g + 1]).then_inc(oT_ok, 1)

            @block.tensor
            def _(t):
                t.wait_ge(sel_ok, 2)
                for n, (b, g) in enumerate(steps):
                    for c in range(NST):
                        h = g * G + c // 2
                        at = b * SEQ + (c % 2) * NT
                        if c or n:
                            t.wait_ge(q_ok, n * NST + c)
                            t.wait_ge(k_ok, n * NST + c)
                        for a_ in range(2):
                            if a_ == 0 and c == 0 and n:
                                t.wait_ge(qm_ok, 2 * G * n)
                            t.matmul(st[:, a_, :], sel[:, 2 * a_, h, :], o.hi[:, a_, at:at + NT], start=True, stop=False)
                            t.matmul(st[:, a_, :], sel[:, 2 * a_ + 1, h, :], o.lo[:, a_, at:at + NT], start=False, stop=True).then_inc(stacked, 1)
                    t.wait_ge(q_ok, (n + 1) * NST)
                    t.wait_ge(k_ok, (n + 1) * NST)
                    if n:
                        t.wait_ge(o_ok, n)
                    for h in range(G):
                        for qt in range(KTS):
                            m = (n * G + h) * KTS + qt
                            if qt or h:
                                t.wait_ge(max_ok, m - 1)
                            for c in range(2):
                                last = t.matmul(S[:, m % 2, c * NT:(c + 1) * NT], Q[:, h, qt * P:(qt + 1) * P], Kk[:, h, c * NT:(c + 1) * NT],
                                                start=True, stop=True)
                            last.then_inc(s1, 1)
                        m = n * G + h
                        t.wait_ge(mz_ok, 2 * (m + 1))
                        for c in range(2):
                            if m:
                                t.wait_ge(qm_ok, 2 * m)
                            for j in range(KTS // 2):
                                last = t.transpose(st[:, c, j * P:(j + 1) * P], mz[:, c * (KTS // 2) + j, :], K.ident[:, :])
                            last.then_inc(mT, 1)
                    t.wait_ge(qm_ok, 2 * G * (n + 1))
                    t.wait_ge(max_ok, (n + 1) * G * KTS)
                    if n:
                        t.wait_ge(osb_ok, n)
                    for kt in range(KTS + 1):
                        if kt < KTS:
                            for h in range(G):
                                m = (n * KTS + kt) * G + h
                                if kt or h:
                                    t.wait_ge(exp_ok, m - 1) if (m - 1) > 0 else None
                                for c in range(2):
                                    last = t.matmul(S[:, m % 2, c * NT:(c + 1) * NT], Kk[:, h, kt * P:(kt + 1) * P], Q[:, h, c * NT:(c + 1) * NT],
                                                    start=True, stop=True)
                                last.then_inc(s2, 1)
                        if kt:
                            j = kt - 1
                            t.wait_ge(exp_ok, (n * KTS + j + 1) * G)
                            for c in range(2):
                                for h in range(G):
                                    last = t.matmul(O[HP * h:HP * h + HP, c * NT:(c + 1) * NT], o.v[:, b * KTS + j, g * G + h, :],
                                                    PT[:, (j * G + h) % RING, c * NT:(c + 1) * NT], start=j == 0, stop=j == KTS - 1)
                            last.then_inc(pv, 1)
                    t.wait_ge(osb_ok, n + 1)
                    for c in range(2):
                        last = t.matmul(S[:, 0, c * NT:(c + 1) * NT], sumsel[:, :], osb[:, c * NT:(c + 1) * NT], start=True, stop=True)
                    last.then_inc(bsum, 1)


class L0Out(DenseLN):

    def __init__(self, s, K, w, oT):
        super().__init__(s, K)
        self.w, self.oT = w, oT
        self.idx = s.sb("idx", [P, KT], I32)
        self.rows = s.sb("rows", [P, KT, GROUPS * P + 1])
        self.W = s.sb("W", [P, GROUPS, D])
        self.tp = s.ps("tp", [P, 2, NT])
        self.idx_in = s.sem("idx_in")
        self.rows_in = [s.sem(f"rows_in{k}") for k in range(KT)]
        self.turned = s.sem("turned")
        self.w_ok = s.sem("w_ok")

    def sync(self, e):
        e.dma_start(self.idx[:, :], self.w["perm"]).then_inc(self.idx_in, 16)

    def gpsimd(self, g):
        g.wait_ge(self.idx_in, 16)
        for k in range(KT):
            g.indirect_dma_start(out=self.rows[:, k, :], out_offset=None, in_=self.w["wo_rows"],
                                 in_offset=bass.IndirectOffsetOnAxis(ap=self.idx[:, k:k + 1].bitcast(U32), axis=0)).then_inc(self.rows_in[k], 16)

    def t_start(self, t):
        for k in range(KT):
            t.wait_ge(self.rows_in[k], 16)
            for g in range(GROUPS):
                n = k * GROUPS + g
                if n >= 2:
                    t.wait_ge(self.w_ok, n - 1)
                t.transpose(self.tp[:, n % 2, 0:P], self.rows[:, k, g * P:(g + 1) * P], self.K.ident[:, :]).then_inc(self.turned, 1)
        t.wait_ge(self.w_ok, KT * GROUPS)

    def a_start(self, a):
        for k in range(KT):
            for g in range(GROUPS):
                n = k * GROUPS + g
                a.wait_ge(self.turned, n + 1)
                a.activation(self.W[:, g, k * P:(k + 1) * P], self.tp[:, n % 2, 0:P], ACT.Copy).then_inc(self.w_ok, 1)

    def v_start(self, v):
        for k in range(KT):
            v.wait_ge(self.rows_in[k], 16)

    def t_tile(self, t, i, m, acc):
        for g in range(GROUPS):
            last = t.matmul(acc, self.W[:, g, m * P:(m + 1) * P], self.oT[:, g, i * NT:(i + 1) * NT], start=g == 0, stop=g == GROUPS - 1)
        return last

    def v_tile(self, v, i, m, acc, z, x):
        return v.scalar_tensor_tensor(z, acc, self.rows[:, m, GROUPS * P:], x, ALU.add, ALU.add)


class Buffers:
    pass


def l0_attn(nc, K, w):
    with Stage(nc, "l0") as s:
        o = Buffers()
        o.oT = s.sb("oT", [P, GROUPS, T])
        with Stage(nc, "l0qkv") as s1:
            o.hi = s1.sb("hi", [P, 2, T], F32R)
            o.lo = s1.sb("lo", [P, 2, T], F32R)
            o.v = s1.sb("v", [P, T // P, HEADS, HP])
            a = L0Attn(nc, K, w)
            with Stage(nc, "l0proj") as s2:
                a.project(s2, o)
            with Stage(nc, "l0att") as s2:
                a.attend(s2, o)
        with Stage(nc, "l0out") as s1:
            L0Out(s1, K, w, o.oT).run(nc)


def host_l0attn(i, x):
    wqk = i['L0_attn_Wqk_w'].reshape(HD, 2, D)
    bqk = i['L0_attn_Wqk_b'].reshape(HD, 2)
    wo = np.zeros((D, GROUPS, G, HP), np.float32)
    wo[..., :HE] = i['L0_attn_Wo_w'].reshape(D, GROUPS, G, HE)
    vb = np.zeros((GROUPS, G, HP), np.float32)
    vb[..., :HE] = i['L0_attn_Wv_b'].reshape(GROUPS, G, HE)
    return dict(perm=i['L0_ffn_perm'].reshape(KT, P).T, x_rows=x.T.reshape(D * BATCH, SEQ),
                qkv_T=np.concatenate([wqk[:, 0].T, wqk[:, 1].T, i['L0_attn_Wv_w'].T], 1),
                qk_b=bqk, v_b=vb.reshape(GROUPS, P).T,
                wo_rows=np.concatenate([wo.reshape(D, GROUPS * P), i['L0_attn_Wo_b'].reshape(D, 1)], 1))



class L0Ffn(DenseLN):
    H, DH, M = 16, 64, 256
    MT = M // P

    def __init__(self, s, K, w):
        super().__init__(s, K, acc=2)
        self.w = w
        self.up = s.sb("up", [P, KT, 2, self.M])
        self.down = s.sb("down", [P, self.H, self.MT, self.DH])
        self.g = s.sb("g", [P, 2, 2, self.MT, NT])
        self.ups = s.ps("ups", [P, 2, self.MT, NT])
        self.zeroed = s.sem("zeroed")
        self.up_in = s.sem("up_in")
        self.down_in = s.sem("down_in")
        self.up_ready = s.sem("up_ready")
        self.g_ok = s.sem("g_ok")

    def gpsimd(self, g):
        g.memset(self.up[0:self.DH, :, 1, :], 0.0).then_inc(self.zeroed, 1)
        g.memset(self.up[self.DH:P, :, 0, :], 0.0).then_inc(self.zeroed, 1)

    def sync(self, e):
        u = self.w["up"].rearrange("(m j) d n -> j d m n", j=2)
        e.dma_start(self.up[0:self.DH, :, 0, :], u[0]).then_inc(self.up_in, 16)
        e.dma_start(self.up[self.DH:P, :, 1, :], u[1]).then_inc(self.up_in, 16)
        e.dma_start(self.down[:, :, :, :], self.w["down"]).then_inc(self.down_in, 16)

    def t_up(self, t, n):
        i, m = divmod(n, KT)
        x = cols(self.K.X, i)
        for j in range(2):
            if n:
                t.wait_ge(self.g_ok, 2 * (n - 1) + j + 1)
            for q in range(self.MT):
                last = t.matmul(self.ups[:, j, q, :], self.up[:, m, j, q * P:(q + 1) * P], x[:, m, :], start=True, stop=True)
            last.then_inc(self.up_ready, 1)

    def t_start(self, t):
        t.wait_ge(self.zeroed, 2)
        t.wait_ge(self.up_in, 32)
        self.t_up(t, 0)
        t.wait_ge(self.down_in, 16)

    def t_tile(self, t, i, m, acc):
        n = i * KT + m
        if n + 1 < CHUNKS * KT:
            self.t_up(t, n + 1)
        t.wait_ge(self.g_ok, 2 * n + 2)
        for q in range(self.MT):
            for j in range(2):
                last = t.matmul(acc[j * self.DH:(j + 1) * self.DH, :], self.down[:, 2 * m + j, q, :], self.g[:, n % 2, j, q, :],
                                start=q == 0, stop=q == self.MT - 1)
        return last

    def v_tile(self, v, i, m, acc, z, x):
        return v.tensor_tensor(z, acc, x, ALU.add)

    def scalar(self, a):
        for n in range(CHUNKS * KT):
            i, m = divmod(n, KT)
            for j in range(2):
                a.wait_ge(self.up_ready, 2 * n + j + 1)
                if n >= 2:
                    a.wait_ge(self.acc_ready, n - 1)
                a.activation(self.g[:, n % 2, j], self.ups[:, j], ACT.Gelu).then_inc(self.g_ok, 1)
            if i and m == 2:
                self.ln.a_square(a, i - 1)
            if i and m == 7:
                self.ln.a_std(a, i - 1)
        self.ln.a_square(a, CHUNKS - 1)
        self.ln.a_std(a, CHUNKS - 1)


def unpermute(nc, K, w, scratch):
    with Stage(nc, "unperm") as s:
        idx = s.sb("idx", [P, KT], I32)
        idx2 = s.sb("idx2", [P, KT, BATCH], I32)
        idx_in, idx_ok = s.sem("idx_in"), s.sem("idx_ok")
        out = [s.sem(f"out{b}") for b in range(BATCH)]
        back = s.sem("back")
        with nc.Block() as block:
            @block.vector
            def _(v):
                v.wait_ge(idx_in, 16)
                for b in range(BATCH):
                    v.tensor_scalar(idx2[:, :, b], idx[:, :], float(BATCH), float(b), ALU.mult, ALU.add).then_inc(idx_ok, 1)

            @block.gpsimd
            def _(g):
                g.wait_ge(idx_ok, BATCH)
                for b in range(BATCH):
                    for k in range(KT):
                        g.indirect_dma_start(out=scratch, out_offset=bass.IndirectOffsetOnAxis(ap=idx2[:, k, b:b + 1].bitcast(U32), axis=0),
                                             in_=K.X[:, k, b, PAD:PAD + SEQ], in_offset=None).then_inc(out[b], 16)

            @block.sync
            def _(e):
                e.dma_start(idx[:, :], w["perm"]).then_inc(idx_in, 16)
                rows = scratch.rearrange("(k p b) t -> b p k t", p=P, b=BATCH)
                for b in range(BATCH):
                    e.wait_ge(out[b], 16 * KT)
                    e.dma_start(K.X[:, :, b, PAD:PAD + SEQ], rows[b]).then_inc(back, 16)
                e.wait_ge(back, 16 * BATCH)


def l0_ffn(nc, K, w):
    with Stage(nc, "l0ffn") as s:
        L0Ffn(s, K, w).run(nc)
    scratch = nc.dram_tensor("l0_state_rows", (D * BATCH, SEQ), F32, kind="Internal").ap()
    unpermute(nc, K, w, scratch)


def host_l0ffn(i):
    return dict(up=i['L0_ffn_up'], down=i['L0_ffn_down'].reshape(16, 2, P, 64).transpose(2, 0, 1, 3), perm=i['L0_ffn_perm'].reshape(KT, P).T)



W3 = 256
WK = W3 // P
TAPS = 3
BHEADS, DH = 16, 64
HW = BHEADS * DH
BLK = 128
UNIT = 256
MASKED = -1.0e9


def conv(nc, K, w, qkv):
    M = 3 * W3 // P
    with Stage(nc, "l1conv") as s:
        W = s.sb("W", [P, 2, TAPS, KT, P])
        b = s.sb("b", [P, M])
        acc = s.ps("acc", [P, 4, NT])
        w_in = [s.sem(f"w_in{j}") for j in range(2)]
        b_in = s.sem("b_in")
        acc_ready, acc_ok = s.sem("acc_ready"), s.sem("acc_ok")
        with nc.Block() as block:
            @block.sync
            def _(e):
                e.dma_start(b[:, :], w["conv_b"]).then_inc(b_in, 16)
                for m in range(M):
                    if m >= 2:
                        e.wait_ge(acc_ready, CHUNKS * (m - 1))
                    e.dma_start(W[:, m % 2], w["conv_w"][m]).then_inc(w_in[m % 2], 16)

            @block.tensor
            def _(t):
                for m in range(M):
                    t.wait_ge(w_in[m % 2], 16 * (m // 2 + 1))
                    for i in range(CHUNKS):
                        n = m * CHUNKS + i
                        if n >= 4:
                            t.wait_ge(acc_ok, n - 3)
                        for tap in range(TAPS):
                            x = cols(K.X, i, tap - 1)
                            for k in range(KT):
                                last = t.matmul(acc[:, n % 4, :], W[:, m % 2, tap, k, :], x[:, k, :],
                                                start=tap == 0 and k == 0, stop=tap == TAPS - 1 and k == KT - 1)
                        last.then_inc(acc_ready, 1)

            @block.scalar
            def _(a):
                a.wait_ge(b_in, 16)
                for m in range(M):
                    for i in range(CHUNKS):
                        n = m * CHUNKS + i
                        a.wait_ge(acc_ready, n + 1)
                        a.activation(qkv[:, m, i * NT:(i + 1) * NT], acc[:, n % 4, :], ACT.Identity, bias=b[:, m:m + 1]).then_inc(acc_ok, 1)


def block_attention(nc, K, w, qkv):
    UNITS = T // UNIT
    HH = 8
    STEPS = UNIT // BLK * (BHEADS // HH)
    place = [(h % 2) * (HH // 2) + h // 2 for h in range(HH)]
    with Stage(nc, "l1att") as s:
        wq, wk, wv = (s.sb(n, [P, WK, HW]) for n in ("wq", "wk", "wv"))
        wo = s.sb("wo", [P, HW // P, W3])
        bq, bk, bv = (s.sb(n, [P, HW // P]) for n in ("bq", "bk", "bv"))
        bo = s.sb("bo", [P, WK])
        mask = s.sb("mask", [P, BLK])
        qh = s.sb("qh", [P, HW // P, UNIT])
        kh = s.sb("kh", [P, HW // P, UNIT])
        vh = s.sb("vh", [P, UNIT // BLK, HW])
        oT = s.sb("oT", [P, HW // P, UNIT])
        S = s.sb("S", [P, 2, HH, BLK])
        PT = s.sb("PT", [P, 2, HH, BLK])
        row = s.sb("row", [P, 3, HH])
        pj = s.ps("pj", [P, 3, NT])
        sc = s.ps("sc", [P, HH, BLK])
        tp = s.ps("tp", [P, HH, BLK])
        op = s.ps("op", [P, HH // 2, BLK])
        w_in = s.sem("w_in")
        mask_ok = s.sem("mask_ok")
        pj_ready, pj_ok = s.sem("pj_ready"), s.sem("pj_ok")
        sc_ready, masked = s.sem("sc_ready"), s.sem("masked")
        shifted, exped, p_ok = s.sem("shifted"), s.sem("exped"), s.sem("p_ok")
        turned, pt_ok = s.sem("turned"), s.sem("pt_ok")
        op_ready, oT_ok = s.sem("op_ready"), s.sem("oT_ok")
        order = s.sem("order")
        NQK = 2 * HW // P
        NV = UNIT // BLK * 2
        NPJ = NQK + NV + WK
        with nc.Block() as block:
            @block.sync
            def _(e):
                for dst, name in ((wq, "wq"), (wk, "wk"), (wv, "wv"), (wo, "wo"), (bq, "bq"), (bk, "bk"), (bv, "bv"), (bo, "bo")):
                    e.dma_start(dst[:], w[name]).then_inc(w_in, 16)

            @block.gpsimd
            def _(g):
                g.memset(mask[:, :], 0.0).then_inc(mask_ok, 1)
                g.wait_ge(mask_ok, 1)
                g.affine_select(out=mask[:, :], in_=mask[:, :], compare_op=ALU.is_ge, fill=MASKED, base=0,
                                pattern=[[-1, BLK]], channel_multiplier=1).then_inc(mask_ok, 1)

            @block.tensor
            def _(t):
                n_pj = 0

                def slot():
                    if n_pj >= 3:
                        t.wait_ge(pj_ok, n_pj - 2)
                    return pj[:, n_pj % 3, :]

                def scores(n):
                    u, st = divmod(n, STEPS)
                    blk, half = divmod(st, 2)
                    if n:
                        t.wait_ge(masked, n)
                    for h in range(HH):
                        hh = half * HH + h
                        r = slice((hh % 2) * DH, (hh % 2 + 1) * DH)
                        c = slice(blk * BLK, (blk + 1) * BLK)
                        last = t.matmul(sc[:, place[h], :], qh[r, hh // 2, c], kh[r, hh // 2, c], start=True, stop=True)
                    last.then_inc(sc_ready, 1)

                t.wait_ge(w_in, 16 * 8)
                for u in range(UNITS):
                    at = u * UNIT
                    for j, wt in enumerate((wq, wk)):
                        for m in range(HW // P):
                            o = slot()
                            for k in range(WK):
                                last = t.matmul(o[:, 0:UNIT], wt[:, k, m * P:(m + 1) * P], qkv[:, WK * j + k, at:at + UNIT], start=k == 0, stop=k == WK - 1)
                            last.then_inc(pj_ready, 1)
                            n_pj += 1
                    for blk in range(UNIT // BLK):
                        for half in range(2):
                            o = slot()
                            for k in range(WK):
                                last = t.matmul(o, qkv[:, 2 * WK + k, at + blk * BLK:at + (blk + 1) * BLK], wv[:, k, half * NT:(half + 1) * NT],
                                                start=k == 0, stop=k == WK - 1)
                            last.then_inc(pj_ready, 1)
                            n_pj += 1
                    t.wait_ge(pj_ok, u * NPJ + NQK + NV)
                    scores(u * STEPS)
                    for st in range(STEPS):
                        n = u * STEPS + st
                        blk, half = divmod(st, 2)
                        if st + 1 < STEPS:
                            scores(n + 1)
                        t.wait_ge(p_ok, n + 1)
                        if n:
                            t.wait_ge(pt_ok, n)
                        for h in range(HH):
                            last = t.transpose(tp[:, h, :], S[:, n % 2, h, :], K.ident[:, :])
                        last.then_inc(turned, 1)
                        t.wait_ge(pt_ok, n + 1)
                        if n:
                            t.wait_ge(oT_ok, n)
                        for h in range(HH):
                            hh = half * HH + h
                            last = t.matmul(op[(h % 2) * DH:(h % 2 + 1) * DH, h // 2, :], vh[:, blk, hh * DH:(hh + 1) * DH], PT[:, n % 2, place[h], :],
                                            start=True, stop=True)
                        last.then_inc(op_ready, 1)
                    t.wait_ge(oT_ok, (u + 1) * STEPS)
                    for m in range(WK):
                        o = slot()
                        for k in range(HW // P):
                            last = t.matmul(o[:, 0:UNIT], wo[:, k, m * P:(m + 1) * P], oT[:, k, :], start=k == 0, stop=k == HW // P - 1)
                        last.then_inc(pj_ready, 1)
                        n_pj += 1

            @block.vector
            def _(v):
                link = Chain(v, order).link
                v.wait_ge(mask_ok, 2)
                for n in range(UNITS * STEPS):
                    x = S[:, n % 2]
                    v.wait_ge(sc_ready, n + 1)
                    if n >= 2:
                        v.wait_ge(turned, n - 1)
                    v.scalar_tensor_tensor(x, sc[:, :, :], DH ** -0.5, mask[:, None, :].to_broadcast([P, HH, BLK]), ALU.mult, ALU.add).then_inc(masked, 1)
                    v.wait_ge(masked, n + 1)
                    link(v.tensor_reduce(row[:, 0, :], x, AX.X, ALU.max))
                    v.tensor_tensor(x, x, row[:, 0, :, None].to_broadcast([P, HH, BLK]), ALU.subtract).then_inc(shifted, 1)
                    v.wait_ge(exped, n + 1)
                    link(v.tensor_reduce(row[:, 1, :], x, AX.X, ALU.add))
                    link(v.reciprocal(row[:, 2, :], row[:, 1, :]))
                    v.tensor_tensor(x, x, row[:, 2, :, None].to_broadcast([P, HH, BLK]), ALU.mult).then_inc(p_ok, 1)

            @block.scalar
            def _(a):
                a.wait_ge(w_in, 16 * 8)
                n_pj = 0

                def evac(dst, width, bias=None):
                    nonlocal n_pj
                    a.wait_ge(pj_ready, n_pj + 1)
                    src = pj[:, n_pj % 3, 0:width]
                    (a.activation(dst, src, ACT.Copy) if bias is None else
                     a.activation(dst, src, ACT.Identity, bias=bias)).then_inc(pj_ok, 1)
                    n_pj += 1

                def exp(n):
                    a.wait_ge(shifted, n + 1)
                    a.activation(S[:, n % 2], S[:, n % 2], ACT.Exp).then_inc(exped, 1)

                for u in range(UNITS):
                    for dst, b in ((qh, bq), (kh, bk)):
                        for m in range(HW // P):
                            evac(dst[:, m, :], UNIT, b[:, m:m + 1])
                    for blk in range(UNIT // BLK):
                        for half in range(2):
                            if u and blk == half == 0:
                                a.wait_ge(op_ready, u * STEPS)
                            evac(vh[:, blk, half * NT:(half + 1) * NT], NT)
                    exp(u * STEPS)
                    for st in range(STEPS):
                        n = u * STEPS + st
                        blk, half = divmod(st, 2)
                        if st + 1 < STEPS:
                            exp(n + 1)
                        a.wait_ge(turned, n + 1)
                        a.activation(PT[:, n % 2], tp[:, :, :], ACT.Copy).then_inc(pt_ok, 1)
                        a.wait_ge(op_ready, n + 1)
                        if u and st == 0:
                            a.wait_ge(pj_ready, u * NPJ)
                        for j in range(HH // 2):
                            m = half * (HH // 2) + j
                            last = a.activation(oT[:, m, blk * BLK:(blk + 1) * BLK], op[:, j, :], ACT.Identity, bias=bv[:, m:m + 1])
                        last.then_inc(oT_ok, 1)
                    for m in range(WK):
                        evac(qkv[:, m, u * UNIT:(u + 1) * UNIT], UNIT, bo[:, m:m + 1])


class L1Proj(DenseLN):
    def __init__(self, s, K, w, o):
        super().__init__(s, K)
        self.w, self.o = w, o
        self.W = s.sb("W", [P, WK, D])
        self.b = s.sb("b", [P, KT])
        self.w_in, self.b_in = s.sem("w_in"), s.sem("b_in")

    def sync(self, e):
        e.dma_start(self.W[:, :, :], self.w["proj_w"]).then_inc(self.w_in, 16)
        e.dma_start(self.b[:, :], self.w["proj_b"]).then_inc(self.b_in, 16)

    def v_start(self, v):
        v.wait_ge(self.b_in, 16)

    def t_start(self, t):
        t.wait_ge(self.w_in, 16)

    def t_tile(self, t, i, m, acc):
        for k in range(WK):
            last = t.matmul(acc, self.W[:, k, m * P:(m + 1) * P], self.o[:, k, i * NT:(i + 1) * NT], start=k == 0, stop=k == WK - 1)
        return last

    def v_tile(self, v, i, m, acc, z, x):
        return v.scalar_tensor_tensor(z, acc, self.b[:, m:m + 1], x, ALU.add, ALU.add)


def l1_attn(nc, K, w):
    with Stage(nc, "l1") as s:
        qkv = s.sb("qkv", [P, 3 * WK, T])
        conv(nc, K, w, qkv)
        block_attention(nc, K, w, qkv)
        with Stage(nc, "l1proj") as s1:
            L1Proj(s1, K, w, qkv).run(nc)


def pk(w, k):
    return np.ascontiguousarray(w.reshape(k, P, -1).transpose(1, 0, 2))


def host_l1attn(i):
    cw = i['L1_attn_conv_w']
    return dict(conv_w=cw.reshape(3, KT, P, 6, P).transpose(3, 2, 0, 1, 4), conv_b=i['L1_attn_conv_b'].reshape(6, P).T,
        wq=pk(i['L1_attn_wq'].reshape(W3, HW), WK), wk=pk(i['L1_attn_wk'].reshape(W3, HW), WK), wv=pk(i['L1_attn_wv'].reshape(W3, HW), WK),
        bq=i['L1_attn_bq'].reshape(8, P).T, bk=i['L1_attn_bk'].reshape(8, P).T, bv=i['L1_attn_bv'].reshape(8, P).T,
        wo=pk(i['L1_attn_wo'].reshape(HW, W3), 8), bo=i['L1_attn_bo'].reshape(2, P).T,
        proj_w=pk(i['L1_attn_proj_w'], 2), proj_b=i['L1_attn_proj_b'].reshape(8, P).T)



QT = NT // P


class Router:

    def __init__(self, s, K, E, rT_used, top=None):
        self.s, self.K, self.E, self.top = s, K, E, top
        self.gate = s.sb("gate", [P, KT, E])
        self.gate_b = s.sb("gate_b", [P, E]) if top else None
        self.p = s.sb("p", [P, QT, E])
        self.kept = s.sb("kept", [P, QT, E])
        self.rest = s.sb("rest", [P, QT, E])
        self.best = s.sb("best", [P, QT, 8])
        self.row = s.sb("row", [P, 2, QT])
        self.rT = s.sb("rT", [P, 2, NT])
        self.ps = s.ps("router", [P, NT])
        self.psT = s.ps("routerT", [E, NT])
        self.gate_in = s.sem("gate_in")
        self.zeroed = s.sem("zeroed")
        self.logits = s.sem("logits")
        self.shifted = s.sem("shifted")
        self.exped = s.sem("exped")
        self.probs = s.sem("probs")
        self.turned = s.sem("turned")
        self.rT_ready = s.sem("rT_ready")
        self.rT_used = rT_used

    def t_logits(self, t, j):
        if j == 0:
            t.wait_ge(self.gate_in, 16 * (2 if self.top else 1))
        else:
            t.wait_ge(self.shifted, j)
        x = cols(self.K.X, j)
        for q in range(QT):
            for k in range(KT):
                last = t.matmul(self.ps[:, q * self.E:(q + 1) * self.E], x[:, k, q * P:(q + 1) * P], self.gate[:, k, :],
                                start=k == 0, stop=k == KT - 1)
        last.then_inc(self.logits, 1)

    def v_shift(self, v, j, link):
        E = self.E
        v.wait_ge(self.logits, j + 1)
        if j:
            v.wait_ge(self.turned, j)
        lg = self.ps[:, 0:QT * E].rearrange("p (q e) -> p q e", e=E)
        if self.top:
            v_b = self.gate_b[:, None, :].to_broadcast([P, QT, E])
            link(v.tensor_tensor(self.rest[:, :, :], lg, v_b, ALU.add))
            lg = self.rest[:, :, :]
        link(v.tensor_reduce(self.row[:, 0, :], lg, AX.X, ALU.max))
        v.tensor_tensor(self.p[:, :, :], lg, self.row[:, 0, :, None].to_broadcast([P, QT, E]),
                        ALU.subtract).then_inc(self.shifted, 1)

    def a_exp(self, a, j):
        a.wait_ge(self.shifted, j + 1)
        a.activation(self.p[:, :, :], self.p[:, :, :], ACT.Exp).then_inc(self.exped, 1)

    def v_probs(self, v, j, link):
        E = self.E
        v.wait_ge(self.exped, j + 1)
        link(v.tensor_reduce(self.row[:, 0, :], self.p[:, :, :], AX.X, ALU.add))
        link(v.reciprocal(self.row[:, 1, :], self.row[:, 0, :]))
        r = self.row[:, 1, :, None].to_broadcast([P, QT, E])
        if not self.top:
            v.tensor_tensor(self.kept[:, :, :], self.p[:, :, :], r, ALU.mult).then_inc(self.probs, 1)
            return
        link(v.tensor_tensor(self.p[:, :, :], self.p[:, :, :], r, ALU.mult))
        for q in range(QT):
            link(v.max(self.best[:, q, :], self.p[:, q, :]))
        for q in range(QT):
            link(v.match_replace(out=self.rest[:, q, :], in_to_replace=self.best[:, q, :], in_values=self.p[:, q, :], imm_value=0.0))
        v.tensor_tensor(self.kept[:, :, :], self.p[:, :, :], self.rest[:, :, :], ALU.subtract).then_inc(self.probs, 1)

    def t_turn(self, t, j):
        t.wait_ge(self.probs, j + 1)
        if j:
            t.wait_ge(self.rT_ready, j)
        for q in range(QT):
            last = t.transpose(self.psT[0:self.E, q * P:(q + 1) * P], self.kept[:, q, :], self.K.ident[:, :])
        last.then_inc(self.turned, 1)

    def v_rT(self, v, j):
        v.wait_ge(self.turned, j + 1)
        if j >= 2:
            v.wait_ge(self.rT_used, (j - 1) * KT)
        v.tensor_copy(self.rT[0:self.E, j % 2, :], self.psT[0:self.E, :]).then_inc(self.rT_ready, 1)

    def t_after(self, t, i, m):
        if i + 1 < CHUNKS and m == 1:
            self.t_logits(t, i + 1)
        if i + 1 < CHUNKS and m == 4:
            self.t_turn(t, i + 1)

    def v_after(self, v, i, m, link):
        if i + 1 < CHUNKS and m == 1:
            self.v_shift(v, i + 1, link)
        if i + 1 < CHUNKS and m == 2:
            self.v_probs(v, i + 1, link)
        if i + 1 < CHUNKS and m == 4:
            self.v_rT(v, i + 1)

    def g_zero(self, g, operand):
        g.memset(self.rT[:, :, :], 0.0).then_inc(self.zeroed, 1)
        g.memset(operand, 0.0).then_inc(self.zeroed, 1)

    def v_first(self, v, link):
        v.wait_ge(self.zeroed, 2)
        self.v_shift(v, 0, link)
        self.v_probs(v, 0, link)
        self.v_rT(v, 0)

    def t_first(self, t):
        self.t_logits(t, 0)
        self.t_turn(t, 0)


class L1Ffn(DenseLN):
    E = 8

    def __init__(self, s, K, w):
        super().__init__(s, K, acc=2)
        self.w = w
        self.r = Router(s, K, self.E, self.acc_ready)
        self.W = s.sb("W", [P, KT, D])
        self.b = s.sb("b", [P, KT])
        self.chan = s.sb("chan", [P, 2, D])
        self.xs = s.sb("xs", [P, KT, NT])
        self.os = s.sb("os", [P, 2, NT])
        self.scaleps = s.ps("scaleps", [P, 2, NT])
        self.w_in = [s.sem(f"w_in{k}") for k in range(KT)]
        self.small_in = s.sem("small_in")
        self.signed = s.sem("signed")
        self.insc = s.sem("insc")
        self.xs_ok = s.sem("xs_ok")
        self.outsc = s.sem("outsc")
        self.os_ok = s.sem("os_ok")

    def sync(self, e):
        e.dma_start(self.r.gate[:, :, :], self.w["gate"]).then_inc(self.r.gate_in, 16)
        e.dma_start(self.b[:, :], self.w["bias"]).then_inc(self.small_in, 16)
        e.wait_ge(self.r.zeroed, 2)
        e.dma_start(self.chan[0:self.E, 0, :], self.w["in_channel"]).then_inc(self.small_in, 16)
        e.dma_start(self.chan[0:self.E, 1, :], self.w["out_channel"]).then_inc(self.small_in, 16)
        for k in range(KT):
            e.dma_start(self.W[:, k, :], self.w["weight_T"][k * P:(k + 1) * P, :]).then_inc(self.w_in[k], 16)

    def gpsimd(self, g):
        self.r.g_zero(g, self.chan[:, :, :])

    def a_start(self, a):
        self.r.a_exp(a, 0)
        for k in range(KT):
            a.wait_ge(self.w_in[k], 16)
            a.activation(self.W[:, k, :], self.W[:, k, :], ACT.Sign).then_inc(self.signed, 1)

    def t_start(self, t):
        self.r.t_first(t)
        t.wait_ge(self.small_in, 48)

    def v_start(self, v):
        v.wait_ge(self.small_in, 48)
        self.r.v_first(v, self.link)

    def t_before(self, t, i):
        t.wait_ge(self.r.rT_ready, i + 1)
        for m in range(KT):
            if i or m:
                t.wait_ge(self.xs_ok, i * KT + m)
            t.matmul(self.scaleps[:, 0, :], self.chan[:, 0, m * P:(m + 1) * P], self.r.rT[:, i % 2, :],
                     start=True, stop=True).then_inc(self.insc, 1)

    def v_before(self, v, i):
        x = cols(self.K.X, i)
        if i:
            v.wait_ge(self.acc_ready, i * KT)
        for m in range(KT):
            v.wait_ge(self.insc, i * KT + m + 1)
            v.tensor_tensor(self.xs[:, m, :], x[:, m, :], self.scaleps[:, 0, :], ALU.mult).then_inc(self.xs_ok, 1)

    def t_tile(self, t, i, m, acc):
        n = i * KT + m
        if n:
            t.wait_ge(self.os_ok, n)
        sc = t.matmul(self.scaleps[:, 1, :], self.chan[:, 1, m * P:(m + 1) * P], self.r.rT[:, i % 2, :],
                      start=True, stop=True)
        sc.then_inc(self.outsc, 1)
        for k in range(KT):
            if n == 0:
                t.wait_ge(self.signed, k + 1)
            if m == 0:
                t.wait_ge(self.xs_ok, i * KT + k + 1)
            last = t.matmul(acc, self.W[:, k, m * P:(m + 1) * P], self.xs[:, k, :], start=k == 0, stop=k == KT - 1)
        return last

    def a_os(self, a, i, m):
        n = i * KT + m
        a.wait_ge(self.outsc, n + 1)
        if n >= 2:
            a.wait_ge(self.acc_free, n - 1)
        a.activation(self.os[:, n % 2, :], self.scaleps[:, 1, :], ACT.Copy).then_inc(self.os_ok, 1)

    def v_tile(self, v, i, m, acc, z, x):
        n = i * KT + m
        v.wait_ge(self.os_ok, n + 1)
        self.link(v.tensor_tensor(z, acc, self.os[:, n % 2, :], ALU.mult))
        return v.scalar_tensor_tensor(z, z, self.b[:, m:m + 1], x, ALU.add, ALU.add)

    def t_after(self, t, i, m):
        self.r.t_after(t, i, m)

    def v_after(self, v, i, m):
        self.r.v_after(v, i, m, self.link)

    def scalar(self, a):
        self.a_start(a)
        for i in range(CHUNKS):
            for m in range(KT):
                self.a_os(a, i, m)
                if i and m == 1:
                    self.ln.a_square(a, i - 1)
                if i + 1 < CHUNKS and m == 3:
                    self.r.a_exp(a, i + 1)
                if i and m == 6:
                    self.ln.a_std(a, i - 1)
        self.ln.a_square(a, CHUNKS - 1)
        self.ln.a_std(a, CHUNKS - 1)


def l1_ffn(nc, K, w):
    with Stage(nc, "l1ffn") as s:
        L1Ffn(s, K, w).run(nc)


def fm(w):
    return np.ascontiguousarray(w.reshape(KT, P, -1).transpose(1, 0, 2))


def host_l1ffn(i):
    return dict(gate=fm(i['L1_ffn_gate_w'].T), bias=i['L1_ffn_bias'].reshape(8,128).T, in_channel=i['L1_ffn_in_channel_scale'],
        out_channel=i['L1_ffn_out_channel_scale'], weight_T=i['L1_ffn_weight'].T)


class L3Ffn(DenseLN):
    N, E, R = 15, 8, 16
    SCALING = 2.0

    def __init__(self, s, K, w):
        super().__init__(s, K, acc=2)
        self.w = w
        self.r = Router(s, K, self.N, self.acc_ready, top=8)
        self.W = s.sb("W", [P, KT, D])
        self.A = s.sb("A", [P, KT, P])
        self.B = s.sb("B", [P, D])
        self.b = s.sb("b", [P, KT])
        self.map_i = s.sb("map_i", [self.N, 1], I32)
        self.map = s.sb("map", [self.N, 1])
        self.expert = s.sb("expert", [self.N, P])
        self.spread = s.sb("spread", [P, P])
        self.w_er = s.sb("w_er", [P, NT])
        self.hw = s.sb("hw", [P, 2, NT])
        self.loraps = s.ps("loraps", [P, 2, NT])
        self.w_in = [s.sem(f"w_in{k}") for k in range(KT)]
        self.small_in = s.sem("small_in")
        self.ab_in = s.sem("ab_in")
        self.iota_ok = s.sem("iota_ok")
        self.spread_ok = s.sem("spread_ok")
        self.er = s.sem("er")
        self.er_ok = s.sem("er_ok")
        self.h = s.sem("h")
        self.hw_ok = s.sem("hw_ok")

    def sync(self, e):
        e.dma_start(self.r.gate[:, :, :], self.w["router"]).then_inc(self.r.gate_in, 16)
        e.dma_start(self.r.gate_b[:, :], self.w["router_b"].to_broadcast([P, self.N])).then_inc(self.r.gate_in, 16)
        e.dma_start(self.b[:, :], self.w["base_b"]).then_inc(self.small_in, 16)
        e.dma_start(self.map_i[:, :], self.w["expert_map"]).then_inc(self.small_in, 16)
        e.dma_start(self.A[:, :, :], self.w["A"]).then_inc(self.ab_in, 16)
        e.dma_start(self.B[:, :], self.w["B"]).then_inc(self.ab_in, 16)
        for k in range(KT):
            e.dma_start(self.W[:, k, :], self.w["base_T"][k * P:(k + 1) * P, :]).then_inc(self.w_in[k], 16)

    def gpsimd(self, g):
        self.r.g_zero(g, self.spread[:, :])
        g.iota(self.expert[:, :], pattern=[[1, self.E], [0, self.R]], base=0, channel_multiplier=0,
               allow_small_or_imprecise_dtypes=True).then_inc(self.iota_ok, 1)

    def a_start(self, a):
        self.r.a_exp(a, 0)

    def t_start(self, t):
        self.r.t_first(t)
        t.wait_ge(self.ab_in, 32)
        t.wait_ge(self.spread_ok, 1)

    def v_start(self, v):
        v.wait_ge(self.small_in, 32)
        v.wait_ge(self.r.gate_in, 32)
        v.wait_ge(self.iota_ok, 1)
        self.link(v.tensor_copy(self.map[:, :], self.map_i[:, :]))
        v.wait_ge(self.r.zeroed, 2)
        v.tensor_scalar(self.spread[0:self.N, :], self.expert[:, :], self.map[:, 0:1], None, ALU.is_equal).then_inc(self.spread_ok, 1)
        self.r.v_first(v, self.link)

    def t_before(self, t, i):
        t.wait_ge(self.r.rT_ready, i + 1)
        if i:
            t.wait_ge(self.er_ok, i)
            t.wait_ge(self.hw_ok, i)
        t.matmul(self.loraps[:, 0, :], self.spread[:, :], self.r.rT[:, i % 2, :], start=True, stop=True).then_inc(self.er, 1)
        x = cols(self.K.X, i)
        for k in range(KT):
            last = t.matmul(self.loraps[:, 1, :], self.A[:, k, :], x[:, k, :], start=k == 0, stop=k == KT - 1)
        last.then_inc(self.h, 1)

    def a_before(self, a, i):
        a.wait_ge(self.er, i + 1)
        if i:
            a.wait_ge(self.hw_ok, i)
        a.activation(self.w_er[:, :], self.loraps[:, 0, :], ACT.Copy, scale=self.SCALING).then_inc(self.er_ok, 1)

    def a_after(self, a, i):
        if i + 1 < CHUNKS:
            self.r.a_exp(a, i + 1)

    def v_before(self, v, i):
        v.wait_ge(self.h, i + 1)
        v.wait_ge(self.er_ok, i + 1)
        if i >= 2:
            v.wait_ge(self.acc_ready, (i - 1) * KT)
        v.tensor_tensor(self.hw[:, i % 2, :], self.loraps[:, 1, :], self.w_er[:, :], ALU.mult).then_inc(self.hw_ok, 1)

    def t_tile(self, t, i, m, acc):
        x = cols(self.K.X, i)
        for k in range(KT):
            if i == m == 0:
                t.wait_ge(self.w_in[k], 16)
            t.matmul(acc, self.W[:, k, m * P:(m + 1) * P], x[:, k, :], start=k == 0, stop=False)
        if m == 0:
            t.wait_ge(self.hw_ok, i + 1)
        return t.matmul(acc, self.B[:, m * P:(m + 1) * P], self.hw[:, i % 2, :], start=False, stop=True)

    def v_tile(self, v, i, m, acc, z, x):
        return v.scalar_tensor_tensor(z, acc, self.b[:, m:m + 1], x, ALU.add, ALU.add)

    def t_after(self, t, i, m):
        if i + 1 < CHUNKS and m == 1:
            self.r.t_logits(t, i + 1)
        if i + 1 < CHUNKS and m == 7:
            self.r.t_turn(t, i + 1)

    def v_after(self, v, i, m):
        if i + 1 < CHUNKS and m == 1:
            self.r.v_shift(v, i + 1, self.link)
        if i + 1 < CHUNKS and m == 6:
            self.r.v_probs(v, i + 1, self.link)
        if i + 1 < CHUNKS and m == 7:
            self.r.v_rT(v, i + 1)


def l3_ffn(nc, K, w):
    with Stage(nc, "l3ffn") as s:
        L3Ffn(s, K, w).run(nc)


def host_l3ffn(i):
    return dict(router=fm(i['L3_ffn_router_W'].T), router_b=i['L3_ffn_router_b'].reshape(1,15), base_b=i['L3_ffn_base_b'].reshape(8,128).T,
        expert_map=i['L3_ffn_expert_map'].reshape(15,1), A=fm(i['L3_ffn_A'].reshape(128,1024).T), B=i['L3_ffn_B'].transpose(0,2,1).reshape(128,1024),
        base_T=i['L3_ffn_base_W'].T)



DIN = 2048
CT = DIN // P
NS = 16
R = 64
TAP = 4
B_AT, C_AT = 64, 96
NG = 4
GR = NS // NG


def l2_inproj(nc, K, w, xc_dram, ssm_dram):
    with Stage(nc, "l2in") as s:
        W = s.sb("W", [P, 2, KT, P])
        Wx = s.sb("Wx", [P, CT, P])
        cw = s.sb("cw", [P, CT, TAP])
        cb = s.sb("cb", [P, CT])
        lnw = s.sb("lnw", [P, 1])
        meanw = s.sb("meanw", [P, P])
        xp = s.sb("xp", [P, 2, BATCH, TAP - 1 + SEQ])
        cv = s.sb("cv", [P, BATCH, SEQ])
        xc = s.sb("xc", [P, 2, BATCH, SEQ])
        sq = s.sb("sq", [P, CHUNKS, NT])
        rs = s.sb("rs", [P, CHUNKS, NT])
        acc = s.ps("acc", [P, 4, NT])
        ssm = s.ps("ssm", [P, CHUNKS, NT])
        w_in = [s.sem(f"w_in{j}") for j in range(2)]
        small_in = s.sem("small_in")
        meanw_ok, pad_ok = s.sem("meanw_ok"), s.sem("pad_ok")
        acc_ready, xp_ok = s.sem("acc_ready"), s.sem("xp_ok")
        tap0, conved, silu_ok = s.sem("tap0"), s.sem("conved"), s.sem("silu_ok")
        projected, stored = s.sem("projected"), [s.sem(f"stored{j}") for j in range(2)]
        sq_ok, ms, std_ok, ssm_ok, ssm_out = (s.sem(x) for x in ("sq_ok", "ms", "std_ok", "ssm_ok", "ssm_out"))
        order = s.sem("order")
        with nc.Block() as block:
            @block.sync
            def _(e):
                for j in range(2):
                    e.dma_start(W[:, j], w["in_x"][j]).then_inc(w_in[j], 16)
                for dst, name in ((cw, "conv_w"), (cb, "conv_b"), (lnw, "ln_w"), (Wx, "x_proj")):
                    e.dma_start(dst[:], w[name]).then_inc(small_in, 16)
                for ct in range(CT):
                    if ct + 2 < CT:
                        e.wait_ge(acc_ready, CHUNKS * (ct + 1))
                        e.dma_start(W[:, ct % 2], w["in_x"][ct + 2]).then_inc(w_in[ct % 2], 16)
                    e.wait_ge(silu_ok, ct + 1)
                    e.dma_start(xc_dram[ct].rearrange("p (b t) -> p b t", b=BATCH), xc[:, ct % 2]).then_inc(stored[ct % 2], 16)
                e.wait_ge(ssm_ok, 1)
                e.dma_start(ssm_dram.rearrange("p (c t) -> p c t", t=NT), sq[:, :, :]).then_inc(ssm_out, 16)
                e.wait_ge(ssm_out, 16)
                for j in range(2):
                    e.wait_ge(stored[j], 16 * CT // 2)

            @block.gpsimd
            def _(g):
                g.memset(meanw[:, :], 0.0).then_inc(meanw_ok, 1)
                for j in range(2):
                    g.memset(xp[:, j, :, 0:TAP - 1], 0.0).then_inc(pad_ok, 1)
                g.wait_ge(pad_ok, 2)
                g.wait_ge(meanw_ok, 1)
                g.memset(meanw[0:R, 0:R], 1.0 / R).then_inc(meanw_ok, 1)
                g.wait_ge(meanw_ok, 2)
                g.memset(meanw[B_AT:B_AT + 32, B_AT:B_AT + NS], 1.0 / NS).then_inc(meanw_ok, 1)
                g.wait_ge(meanw_ok, 3)
                g.memset(meanw[C_AT:C_AT + 32, C_AT:C_AT + NS], 1.0 / NS).then_inc(meanw_ok, 1)

            @block.tensor
            def _(t):
                def project(ct):
                    t.wait_ge(silu_ok, ct + 1)
                    for i in range(CHUNKS):
                        b, h = divmod(i, SEQ // NT)
                        last = t.matmul(ssm[:, i, :], Wx[:, ct, :], xc[:, ct % 2, b, h * NT:(h + 1) * NT], start=ct == 0, stop=ct == CT - 1)
                    last.then_inc(projected, 1)

                t.wait_ge(small_in, 64)
                for ct in range(CT):
                    t.wait_ge(w_in[ct % 2], 16 * (ct // 2 + 1))
                    for i in range(CHUNKS):
                        n = ct * CHUNKS + i
                        if n >= 4:
                            t.wait_ge(xp_ok, n - 3)
                        x = cols(K.X, i)
                        for k in range(KT):
                            last = t.matmul(acc[:, n % 4, :], W[:, ct % 2, k, :], x[:, k, :], start=k == 0, stop=k == KT - 1)
                        last.then_inc(acc_ready, 1)
                    if ct:
                        project(ct - 1)
                project(CT - 1)
                t.wait_ge(meanw_ok, 4)
                t.wait_ge(xp_ok, CT * CHUNKS)
                for i in range(CHUNKS):
                    t.wait_ge(sq_ok, i + 1)
                    t.matmul(acc[:, i, :], meanw[:, :], sq[:, i, :], start=True, stop=True).then_inc(ms, 1)

            @block.scalar
            def _(a):
                a.wait_ge(small_in, 64)
                a.wait_ge(pad_ok, 2)

                def silu(ct):
                    a.wait_ge(conved, ct + 1)
                    if ct >= 2:
                        a.wait_ge(projected, ct - 1)
                        a.wait_ge(stored[ct % 2], 16 * (ct // 2))
                    a.activation(xc[:, ct % 2], cv[:, :, :], ACT.Silu).then_inc(silu_ok, 1)

                for ct in range(CT):
                    for i in range(CHUNKS):
                        n = ct * CHUNKS + i
                        b, h = divmod(i, SEQ // NT)
                        if i == 0 and ct >= 2:
                            a.wait_ge(conved, ct - 1)
                        a.wait_ge(acc_ready, n + 1)
                        at = TAP - 1 + h * NT
                        a.activation(xp[:, ct % 2, b, at:at + NT], acc[:, n % 4, :], ACT.Copy).then_inc(xp_ok, 1)
                    if ct:
                        silu(ct - 1)
                silu(CT - 1)
                a.wait_ge(projected, CT)
                for i in range(CHUNKS):
                    a.activation(sq[:, i, :], ssm[:, i, :], ACT.Square).then_inc(sq_ok, 1)
                for i in range(CHUNKS):
                    a.wait_ge(ms, i + 1)
                    a.activation(rs[:, i, :], acc[:, i, :], ACT.Sqrt, bias=K.eps6[:, :]).then_inc(std_ok, 1)

            @block.vector
            def _(v):
                link = Chain(v, order).link
                v.wait_ge(small_in, 64)
                for ct in range(CT):
                    v.wait_ge(xp_ok, (ct + 1) * CHUNKS)
                    if ct:
                        v.wait_ge(silu_ok, ct)
                    x = xp[:, ct % 2]
                    link(v.tensor_scalar(cv[:, :, :], x[:, :, 0:SEQ], cw[:, ct, 0:1], cb[:, ct:ct + 1], ALU.mult, ALU.add))
                    for j in range(1, TAP):
                        ins = v.scalar_tensor_tensor(cv[:, :, :], x[:, :, j:j + SEQ], cw[:, ct, j:j + 1], cv[:, :, :], ALU.mult, ALU.add)
                        if j < TAP - 1:
                            link(ins)
                    ins.then_inc(conved, 1)
                v.wait_ge(std_ok, CHUNKS)
                link(v.reciprocal(rs[:, :, :], rs[:, :, :]))
                v.scalar_tensor_tensor(sq[:, :, :], ssm[:, :, :], lnw[:, 0:1], rs[:, :, :], ALU.mult, ALU.mult).then_inc(ssm_ok, 1)


def l2_scan(nc, K, w, xc_dram, ssm_dram, y_dram):
    SLOTS = 3
    DT_AT, EXP_AT, LOW_AT, DT_SUM_AT = 1, 0, 1, 1
    with Stage(nc, "l2scan") as s:
        Bb = s.sb("Bb", [P, NS, NT])
        Cb = s.sb("Cb", [P, NS, NT])
        Wz = s.sb("Wz", [P, 2, KT, P])
        Wdt = s.sb("Wdt", [P, 2, P])
        A = s.sb("A", [P, CT, NS])
        dtb = s.sb("dtb", [P, CT])
        Dp = s.sb("Dp", [P, CT])
        carry = s.sb("carry", [P, CT, NS])
        ssm = s.sb("ssm", [P, 2, NT])
        xc = s.sb("xc", [P, 2, NT])
        dt = s.sb("dt", [P, 2, NT])
        dtx = s.sb("dtx", [P, NT])
        zs = s.sb("zs", [P, 2, NT])
        u = s.sb("u", [P, NT])
        l = s.sb("l", [P, NT])
        r = s.sb("r", [P, NT])
        c_ = s.sb("c", [P, NT])
        dA = s.sb("dA", [P, SLOTS, NG, NT])
        h = s.sb("h", [P, 2, NG, NT])
        dtp = s.ps("dtp", [P, 2, NT])
        zp = s.ps("zp", [P, 2, NT])
        yp = s.ps("yp", [P, 2, NT])
        small_in = s.sem("small_in")
        a_ok = s.sem("a_ok")
        w_in = [s.sem(f"w_in{j}") for j in range(2)]
        xc_in = [s.sem(f"xc_in{j}") for j in range(2)]
        ssm_in = [s.sem(f"ssm_in{j}") for j in range(2)]
        bc_in = [s.sem(f"bc_in{g}") for g in range(GR)]
        dt_ready, z_ready = s.sem("dt_ready"), s.sem("z_ready")
        absd, u_ok, l_ok, r_ok = (s.sem(x) for x in ("absd", "u_ok", "l_ok", "r_ok"))
        c_ok, lr_ok, dt_ok, dtx_ok, z_ok = (s.sem(x) for x in ("c_ok", "lr_ok", "dt_ok", "dtx_ok", "z_ok"))
        dA_ok, dBx_ok, h_ok, hC_ok, summed, carried = (s.sem(x) for x in ("dA_ok", "dBx_ok", "h_ok", "hC_ok", "summed", "carried"))
        y_ok = s.sem("y_ok")
        y_out = [s.sem(f"y_out{j}") for j in range(2)]
        order = s.sem("order")
        ITEMS = CHUNKS * CT
        with nc.Block() as block:
            @block.sync
            def _(e):
                def weights(q):
                    ct = q % CT
                    if q >= 2:
                        e.wait_ge(z_ready, q - 1)
                        e.wait_ge(dt_ready, q - 1)
                    e.dma_start(Wz[:, q % 2], w["in_z"][ct]).then_inc(w_in[q % 2], 16)
                    e.dma_start(Wdt[:, q % 2, :], w["dt_proj"][:, ct * P:(ct + 1) * P]).then_inc(w_in[q % 2], 16)

                def channels(q):
                    c, ct = divmod(q, CT)
                    e.dma_start(xc[:, q % 2, :], xc_dram[ct][:, c * NT:(c + 1) * NT]).then_inc(xc_in[q % 2], 16)

                def low_rank(c):
                    e.dma_start(ssm[:, c % 2, :], ssm_dram[:, c * NT:(c + 1) * NT]).then_inc(ssm_in[c % 2], 16)

                def bc(c, g):
                    if c:
                        e.wait_ge(hC_ok, (c * CT - 1) * GR + g + 1)
                    for dst, at in ((Bb, B_AT), (Cb, C_AT)):
                        src = ssm_dram[at + g * NG:at + (g + 1) * NG, c * NT:(c + 1) * NT]
                        e.dma_start(dst[:, g * NG:(g + 1) * NG, :], src[None, :, :].to_broadcast([P, NG, NT])).then_inc(bc_in[g], 16)

                low_rank(0)
                for dst, name in ((A, "A_log"), (dtb, "dt_bias"), (Dp, "D")):
                    e.dma_start(dst[:], w[name]).then_inc(small_in, 16)
                weights(0)
                channels(0)
                for g in range(GR):
                    bc(0, g)
                weights(1)
                channels(1)
                low_rank(1)
                for q in range(ITEMS):
                    c, ct = divmod(q, CT)
                    if q + 2 < ITEMS:
                        weights(q + 2)
                    if q:
                        e.wait_ge(y_ok, q)
                        p = q - 1
                        e.dma_start(y_dram[p % CT][:, p // CT * NT:(p // CT + 1) * NT], zs[:, p % 2, :]).then_inc(y_out[p % 2], 16)
                        if q + 1 < ITEMS:
                            channels(q + 1)
                    if ct == CT - 1 and c + 1 < CHUNKS:
                        for g in range(GR):
                            bc(c + 1, g)
                    if ct == 0 and c and c + 1 < CHUNKS:
                        low_rank(c + 1)
                e.wait_ge(y_ok, ITEMS)
                p = ITEMS - 1
                e.dma_start(y_dram[p % CT][:, p // CT * NT:(p // CT + 1) * NT], zs[:, p % 2, :]).then_inc(y_out[p % 2], 16)
                for j in range(2):
                    e.wait_ge(y_out[j], 16 * ITEMS // 2)

            @block.tensor
            def _(t):
                def dt_tile(q):
                    c, ct = divmod(q, CT)
                    t.wait_ge(w_in[q % 2], 32 * (q // 2 + 1))
                    if ct == 0:
                        t.wait_ge(ssm_in[c % 2], 16 * (c // 2 + 1))
                    if q >= 2:
                        t.wait_ge(r_ok, q - 1)
                    t.matmul(dtp[:, q % 2, :], Wdt[:, q % 2, :], ssm[:, c % 2, :], start=True, stop=True).then_inc(dt_ready, 1)

                def z_part(q, g):
                    c = q // CT
                    if g == 0 and q >= 2:
                        t.wait_ge(z_ok, q - 1)
                    x = cols(K.X, c)
                    for k in range(g * KT // GR, (g + 1) * KT // GR):
                        last = t.matmul(zp[:, q % 2, :], Wz[:, q % 2, k, :], x[:, k, :], start=k == 0, stop=k == KT - 1)
                    if g == GR - 1:
                        last.then_inc(z_ready, 1)

                dt_tile(0)
                dt_tile(1)
                for g in range(GR):
                    z_part(0, g)
                for q in range(ITEMS):
                    if q >= 2:
                        t.wait_ge(y_ok, q - 1)
                    for g in range(GR):
                        st = q * GR + g
                        if q + 1 < ITEMS:
                            z_part(q + 1, g)
                        t.wait_ge(hC_ok, st + 1)
                        for j in range(NG):
                            last = t.matmul(yp[:, q % 2, :], K.ident[:, :], dA[:, st % SLOTS, j, :], start=g == 0 and j == 0, stop=g == GR - 1 and j == NG - 1)
                        last.then_inc(summed, 1)
                        if g == DT_AT and q + 2 < ITEMS:
                            dt_tile(q + 2)

            @block.scalar
            def _(a):
                a.wait_ge(small_in, 48)
                a.activation(A[:, :, :], A[:, :, :], ACT.Exp).then_inc(a_ok, 1)

                def pre(q):
                    ct = q % CT
                    a.wait_ge(dt_ready, q + 1)
                    if q:
                        a.wait_ge(lr_ok, q)
                        a.wait_ge(c_ok, q)
                    a.activation(u[:, :], dtp[:, q % 2, :], ACT.Abs, bias=dtb[:, ct:ct + 1]).then_inc(absd, 1)
                    a.activation(r[:, :], dtp[:, q % 2, :], ACT.Relu, bias=dtb[:, ct:ct + 1]).then_inc(r_ok, 1)
                    a.wait_ge(absd, q + 1)
                    a.activation(u[:, :], u[:, :], ACT.Exp, scale=-1.0).then_inc(u_ok, 1)
                    a.wait_ge(u_ok, q + 1)
                    a.activation(l[:, :], u[:, :], ACT.Ln, bias=K.one[:, :]).then_inc(l_ok, 1)

                def gate(q):
                    a.wait_ge(z_ready, q + 1)
                    if q >= 2:
                        a.wait_ge(y_out[q % 2], 16 * (q // 2))
                    a.activation(zs[:, q % 2, :], zp[:, q % 2, :], ACT.Silu).then_inc(z_ok, 1)

                pre(0)
                a.wait_ge(a_ok, 2)
                for q in range(ITEMS):
                    ct = q % CT
                    for g in range(GR):
                        st = q * GR + g
                        if g == 0:
                            a.wait_ge(dt_ok, q + 1)
                        if st >= SLOTS:
                            a.wait_ge(summed, st - SLOTS + 1)
                        for j in range(NG):
                            n = g * NG + j
                            last = a.activation(dA[:, st % SLOTS, j, :], dt[:, q % 2, :], ACT.Exp, scale=A[:, ct, n:n + 1])
                        last.then_inc(dA_ok, 1)
                        if g == EXP_AT:
                            if q + 1 < ITEMS:
                                pre(q + 1)
                            gate(q)

            @block.gpsimd
            def _(g_):
                def low(q):
                    g_.wait_ge(l_ok, q + 1)
                    g_.wait_ge(r_ok, q + 1)
                    g_.tensor_tensor(l[:, :], l[:, :], r[:, :], ALU.add).then_inc(lr_ok, 1)

                def dtx_(q):
                    g_.wait_ge(dt_ok, q + 1)
                    g_.wait_ge(xc_in[q % 2], 16 * (q // 2 + 1))
                    if q:
                        g_.wait_ge(dBx_ok, q * GR)
                    g_.tensor_tensor(dtx[:, :], dt[:, q % 2, :], xc[:, q % 2, :], ALU.mult).then_inc(dtx_ok, 1)

                low(0)
                dtx_(0)
                for st in range(ITEMS * GR):
                    q, g = divmod(st, GR)
                    c = q // CT
                    if q % CT == 0:
                        g_.wait_ge(bc_in[g], 32 * (c + 1))
                    if g == 0:
                        g_.wait_ge(dtx_ok, q + 1)
                    if st >= 2:
                        g_.wait_ge(hC_ok, st - 1)
                        g_.wait_ge(carried, st - 1)
                    g_.tensor_tensor(h[:, st % 2], dtx[:, None, :].to_broadcast([P, NG, NT]), Bb[:, g * NG:(g + 1) * NG, :],
                                     ALU.mult).then_inc(dBx_ok, 1)
                    if q + 1 < ITEMS and g == LOW_AT:
                        low(q + 1)
                    if q + 1 < ITEMS and g == 3:
                        dtx_(q + 1)

            @block.vector
            def _(v):
                link = Chain(v, order).link
                v.wait_ge(a_ok, 1)
                v.tensor_scalar(A[:, :, :], A[:, :, :], -1.0, None, ALU.mult).then_inc(a_ok, 1)

                def pre(q):
                    v.wait_ge(u_ok, q + 1)
                    if q:
                        v.wait_ge(dt_ok, q)
                    if q >= 2:
                        v.wait_ge(y_ok, q - 1)
                    link(v.tensor_scalar(c_[:, :], u[:, :], 1.0, -1.0, ALU.add, ALU.add))
                    v.tensor_tensor(c_[:, :], u[:, :], c_[:, :], ALU.subtract).then_inc(c_ok, 1)
                    if q >= 2:
                        v.wait_ge(dA_ok, (q - 1) * GR)
                        v.wait_ge(dtx_ok, q - 1)
                    v.wait_ge(lr_ok, q + 1)
                    v.wait_ge(c_ok, q + 1)
                    v.tensor_tensor(dt[:, q % 2, :], l[:, :], c_[:, :], ALU.add).then_inc(dt_ok, 1)

                def finish(q):
                    ct = q % CT
                    v.wait_ge(summed, (q + 1) * GR)
                    v.wait_ge(dt_ok, min(q + 2, ITEMS))
                    link(v.scalar_tensor_tensor(c_[:, :], xc[:, q % 2, :], Dp[:, ct:ct + 1], yp[:, q % 2, :], ALU.mult, ALU.add))
                    z = zs[:, q % 2, :]
                    v.wait_ge(z_ok, q + 1)
                    v.tensor_tensor(z, z, c_[:, :], ALU.mult).then_inc(y_ok, 1)

                pre(0)
                for q in range(ITEMS):
                    c, ct = divmod(q, CT)
                    for g in range(GR):
                        st = q * GR + g
                        v.wait_ge(dA_ok, st + 1)
                        v.wait_ge(dBx_ok, st + 1)
                        if g == 0 and c:
                            v.wait_ge(carried, st - (CT - 1) * GR)
                        for j in range(NG):
                            n = g * NG + j
                            init = carry[:, ct, n:n + 1] if c % (SEQ // NT) else 0.0
                            last = v.tensor_tensor_scan(h[:, st % 2, j, :], dA[:, st % SLOTS, j, :], h[:, st % 2, j, :], init, ALU.mult, ALU.add)
                        last.then_inc(h_ok, 1)
                        v.wait_ge(h_ok, st + 1)
                        v.tensor_copy(carry[:, ct, g * NG:(g + 1) * NG], h[:, st % 2, :, NT - 1]).then_inc(carried, 1)
                        v.tensor_tensor(dA[:, st % SLOTS], h[:, st % 2], Cb[:, g * NG:(g + 1) * NG, :], ALU.mult).then_inc(hC_ok, 1)
                        if g == 1 and q:
                            finish(q - 1)
                        if g == DT_SUM_AT and q + 1 < ITEMS:
                            pre(q + 1)
                finish(ITEMS - 1)


class L2Out(DenseLN):

    def __init__(self, s, K, w, y_dram):
        super().__init__(s, K)
        self.w, self.y_dram = w, y_dram
        self.W = s.sb("W", [P, 2, CT, P])
        self.y = s.sb("y", [P, 2, CT, NT])
        self.w_in = [s.sem(f"w_in{j}") for j in range(2)]
        self.y_in = [s.sem(f"y_in{j}") for j in range(2)]

    def sync(self, e):
        def load_y(i):
            e.dma_start(self.y[:, i % 2], self.y_dram[:, :, i * NT:(i + 1) * NT].rearrange("k p t -> p k t")).then_inc(self.y_in[i % 2], 16)

        def load_w(n):
            e.dma_start(self.W[:, n % 2], self.w["out_w"][n % KT]).then_inc(self.w_in[n % 2], 16)

        load_w(0)
        load_y(0)
        load_w(1)
        load_y(1)
        for n in range(CHUNKS * KT):
            if n + 2 < CHUNKS * KT:
                e.wait_ge(self.acc_ready, n + 1)
                load_w(n + 2)
            if n % KT == KT - 1 and n // KT + 2 < CHUNKS:
                load_y(n // KT + 2)

    def t_tile(self, t, i, m, acc):
        n = i * KT + m
        t.wait_ge(self.w_in[n % 2], 16 * (n // 2 + 1))
        if m == 0:
            t.wait_ge(self.y_in[i % 2], 16 * (i // 2 + 1))
        for k in range(CT):
            last = t.matmul(acc, self.W[:, n % 2, k, :], self.y[:, i % 2, k, :], start=k == 0, stop=k == CT - 1)
        return last

    def v_tile(self, v, i, m, acc, z, x):
        return v.tensor_tensor(z, acc, x, ALU.add)


def l2_attn(nc, K, w):
    xc_dram = nc.dram_tensor("l2_xc", (CT, P, T), F32, kind="Internal").ap()
    ssm_dram = nc.dram_tensor("l2_ssm", (P, T), F32, kind="Internal").ap()
    y_dram = nc.dram_tensor("l2_y", (CT, P, T), F32, kind="Internal").ap()
    l2_inproj(nc, K, w, xc_dram, ssm_dram)
    l2_scan(nc, K, w, xc_dram, ssm_dram, y_dram)
    with Stage(nc, "l2out") as s:
        L2Out(s, K, w, y_dram).run(nc)


def host_l2attn(i):
    wi = i['L2_attn_in_proj_w']
    xpw = np.zeros((DIN, P), np.float32)
    x = i['L2_attn_x_proj_w'].T
    xpw[:, :R] = x[:, :R]; xpw[:, B_AT:B_AT + NS] = x[:, R:R + NS]; xpw[:, C_AT:C_AT + NS] = x[:, R + NS:]
    lnw = np.zeros((P, 1), np.float32)
    lnw[:R, 0] = i['L2_attn_dt_ln_w']; lnw[B_AT:B_AT + NS, 0] = i['L2_attn_B_ln_w']; lnw[C_AT:C_AT + NS, 0] = i['L2_attn_C_ln_w']
    dtp = np.zeros((P, DIN), np.float32)
    dtp[:R] = i['L2_attn_dt_proj_w'].T
    tile = lambda a: a.reshape(KT, P, CT, P).transpose(2, 1, 0, 3)
    chan = lambda a: a.reshape(CT, P, -1).transpose(1, 0, 2)
    return dict(in_x=tile(wi[:, :DIN]), in_z=tile(wi[:, DIN:]), conv_w=chan(i['L2_attn_conv_w']), conv_b=chan(i['L2_attn_conv_b'])[..., 0],
        ln_w=lnw, x_proj=chan(xpw), dt_proj=dtp, A_log=chan(i['L2_attn_A_log']), dt_bias=chan(i['L2_attn_dt_bias'])[..., 0],
        D=chan(i['L2_attn_D_param'])[..., 0], out_w=i['L2_attn_out_proj_w'].T.reshape(CT, P, KT, P).transpose(2, 1, 0, 3))



def unpack_l2_weights(nc, w_packed_T, w_scales_T, perm2, scratch):
    HT = D // 2 // P
    with Stage(nc, "unpack") as s:
        packed = s.sb("packed", [P, 2, D], I32)
        scale = s.sb("scale", [P, 2, D])
        nib = s.sb("nib", [P, 2, D], I32)
        w = s.sb("w", [P, 2, D])
        idx = s.sb("idx", [P, 2, HT], I32)
        loaded = [s.sem(f"loaded{j}") for j in range(2)]
        idx_in = s.sem("idx_in")
        nibbled = s.sem("nibbled")
        made = s.sem("made")
        scattered = [s.sem(f"scattered{j}") for j in range(2)]
        with nc.Block() as block:
            @block.sync
            def _(e):
                e.dma_start(idx[:, :, :], perm2).then_inc(idx_in, 16)
                for t in range(HT):
                    if t >= 2:
                        e.wait_ge(made, 2 * (t - 1))
                    e.dma_start(packed[:, t % 2, :], w_packed_T[t * P:(t + 1) * P, :]).then_inc(loaded[t % 2], 16)
                    for h in range(2):
                        g = 2 * t + h
                        e.dma_start(scale[64 * h:64 * h + 64, t % 2, :],
                                    w_scales_T[g:g + 1, :].to_broadcast([64, D])).then_inc(loaded[t % 2], 16)

            @block.vector
            def _(v):
                for t in range(HT):
                    v.wait_ge(loaded[t % 2], 48 * (t // 2 + 1))
                    for h in range(2):
                        n = 2 * t + h
                        if h == 0:
                            v.tensor_scalar(nib[:, h, :], packed[:, t % 2, :], 15, None, ALU.bitwise_and).then_inc(nibbled, 1)
                        else:
                            v.tensor_scalar(nib[:, h, :], packed[:, t % 2, :], 4, 15, ALU.logical_shift_right, ALU.bitwise_and).then_inc(nibbled, 1)
                        v.wait_ge(nibbled, n + 1)
                        if n >= 2:
                            v.wait_ge(scattered[h], 16 * t)
                        v.scalar_tensor_tensor(w[:, h, :], nib[:, h, :], -8.0, scale[:, t % 2, :], ALU.add, ALU.mult).then_inc(made, 1)

            @block.gpsimd
            def _(g):
                g.wait_ge(idx_in, 16)
                for t in range(HT):
                    for h in range(2):
                        g.wait_ge(made, 2 * t + h + 1)
                        g.indirect_dma_start(out=scratch, out_offset=bass.IndirectOffsetOnAxis(ap=idx[:, h, t:t + 1].bitcast(U32), axis=0),
                                             in_=w[:, h, :], in_offset=None).then_inc(scattered[h], 16)
                for h in range(2):
                    g.wait_ge(scattered[h], 16 * HT)


class L2Ffn(DenseLN):
    def __init__(self, s, K, w_rows, bias):
        super().__init__(s, K)
        self.W = s.sb("W", [P, KT, D])
        self.b = s.sb("b", [P, KT])
        self.w_rows, self.bias = w_rows, bias
        self.w_in = [s.sem(f"w_in{k}") for k in range(KT)]
        self.b_in = s.sem("b_in")

    def sync(self, e):
        e.dma_start(self.b[:, :], self.bias).then_inc(self.b_in, 16)
        for k in range(KT):
            e.dma_start(self.W[:, k, :], self.w_rows[k * P:(k + 1) * P, :]).then_inc(self.w_in[k], 16)

    def v_start(self, v):
        v.wait_ge(self.b_in, 16)

    def t_tile(self, t, i, m, acc):
        x = cols(self.K.X, i)
        for k in range(KT):
            if i == m == 0:
                t.wait_ge(self.w_in[k], 16)
            last = t.matmul(acc, self.W[:, k, m * P:(m + 1) * P], x[:, k, :], start=k == 0, stop=k == KT - 1)
        return last

    def v_tile(self, v, i, m, acc, z, x):
        return v.scalar_tensor_tensor(z, acc, self.b[:, m:m + 1], x, ALU.add, ALU.add)


def l2_ffn(nc, K, w):
    scratch = nc.dram_tensor("l2_rows", (D, D), F32, kind="Internal").ap()
    unpack_l2_weights(nc, w["w_packed_T"], w["w_scales_T"], w["perm2"], scratch)
    with Stage(nc, "l2ffn") as s:
        L2Ffn(s, K, scratch, w["bias"]).run(nc)


def host_l2ffn(i):
    return dict(w_packed_T=i['L2_ffn_w_packed'].T, w_scales_T=i['L2_ffn_w_scales'].T,
        perm2=i['L2_ffn_perm'].reshape(4,128,2).transpose(1,2,0), bias=i['L2_ffn_bias'].reshape(8,128).T)



DA = D // 4
DK = DA // P
QTS = SEQ // P


def l3_project(nc, K, w, qk, vt):
    with Stage(nc, "l3proj") as s:
        W = s.sb("W", [P, KT, 3 * DA])
        b = s.sb("b", [P, 2 * DK])
        acc = s.ps("acc", [P, 4, NT])
        vacc = s.ps("vacc", [P, 2, NT])
        w_in = [s.sem(f"w_in{k}") for k in range(KT)]
        b_in = s.sem("b_in")
        acc_ready, acc_ok, v_ready, v_ok = (s.sem(x) for x in ("acc_ready", "acc_ok", "v_ready", "v_ok"))
        M = 2 * DK
        with nc.Block() as block:
            @block.sync
            def _(e):
                e.dma_start(b[:, :], w["bqk"]).then_inc(b_in, 16)
                for k in range(KT):
                    e.dma_start(W[:, k, :], w["wqkv"][k * P:(k + 1) * P, :]).then_inc(w_in[k], 16)

            @block.tensor
            def _(t):
                for i in range(CHUNKS):
                    x = cols(K.X, i)
                    for m in range(M):
                        n = i * M + m
                        if n >= 4:
                            t.wait_ge(acc_ok, n - 3)
                        for k in range(KT):
                            if n == 0:
                                t.wait_ge(w_in[k], 16)
                            last = t.matmul(acc[:, n % 4, :], W[:, k, m * P:(m + 1) * P], x[:, k, :], start=k == 0, stop=k == KT - 1)
                        last.then_inc(acc_ready, 1)
                    for q in range(NT // P):
                        n = i * (NT // P) + q
                        if n >= 2:
                            t.wait_ge(v_ok, n - 1)
                        for k in range(KT):
                            last = t.matmul(vacc[:, n % 2, 0:DA], x[:, k, q * P:(q + 1) * P], W[:, k, 2 * DA:], start=k == 0, stop=k == KT - 1)
                        last.then_inc(v_ready, 1)

            @block.scalar
            def _(a):
                a.wait_ge(b_in, 16)
                for i in range(CHUNKS):
                    for m in range(M):
                        n = i * M + m
                        a.wait_ge(acc_ready, n + 1)
                        a.activation(qk[:, m, i * NT:(i + 1) * NT], acc[:, n % 4, :], ACT.Identity, bias=b[:, m:m + 1]).then_inc(acc_ok, 1)

            @block.vector
            def _(v):
                for n in range(T // P):
                    v.wait_ge(v_ready, n + 1)
                    v.tensor_copy(vt[:, n, :], vacc[:, n % 2, 0:DA]).then_inc(v_ok, 1)


def l3_attend(nc, K, w, qk, vt, oT):
    with Stage(nc, "l3att") as s:
        bv = s.sb("bv", [P, DK])
        E = s.sb("E", [P, 2, SEQ])
        PT = s.sb("PT", [P, 2, QTS, P])
        row = s.sb("row", [P, 2, 4])
        S = s.ps("S", [P, 2, NT])
        tp = s.ps("tp", [P, QTS, P])
        op = s.ps("op", [P, 2, NT])
        bv_in = s.sem("bv_in")
        sc, nm, exped, e_ok, turned, pt_ok, op_ready, o_ok = (
            s.sem(x) for x in ("sc", "nm", "exped", "e_ok", "turned", "pt_ok", "op_ready", "o_ok"))
        order = s.sem("order")
        N = T // P
        SC = float(DA) ** -0.5
        with nc.Block() as block:
            @block.sync
            def _(e):
                e.dma_start(bv[:, :], w["bv"]).then_inc(bv_in, 16)

            @block.tensor
            def _(t):
                def scores(n):
                    b = n // QTS
                    if n:
                        t.wait_ge(exped, n)
                    for c in range(2):
                        for k in range(DK):
                            last = t.matmul(S[:, c, :], qk[:, k, n * P:(n + 1) * P], qk[:, DK + k, b * SEQ + c * NT:b * SEQ + (c + 1) * NT],
                                            start=k == 0, stop=k == DK - 1)
                    last.then_inc(sc, 1)

                scores(0)
                for n in range(N):
                    b = n // QTS
                    if n + 1 < N:
                        scores(n + 1)
                    t.wait_ge(e_ok, n + 1)
                    if n:
                        t.wait_ge(pt_ok, n)
                    for j in range(QTS):
                        last = t.transpose(tp[:, j, :], E[:, n % 2, j * P:(j + 1) * P], K.ident[:, :])
                    last.then_inc(turned, 1)
                    t.wait_ge(pt_ok, n + 1)
                    if n:
                        t.wait_ge(o_ok, n)
                    for m in range(DK):
                        for j in range(QTS):
                            last = t.matmul(op[:, m, 0:P], vt[:, b * QTS + j, m * P:(m + 1) * P], PT[:, n % 2, j, :], start=j == 0, stop=j == QTS - 1)
                    last.then_inc(op_ready, 1)

            @block.vector
            def _(v):
                link = Chain(v, order).link
                v.wait_ge(bv_in, 16)
                for n in range(N):
                    r = row[:, n % 2, :]
                    v.wait_ge(sc, n + 1)
                    link(v.tensor_reduce(r[:, 0:1], S[:, :, :], AX.XY, ALU.max, negate=True))
                    if n >= 2:
                        v.wait_ge(exped, n - 1)
                    v.tensor_scalar(r[:, 1:2], r[:, 0:1], SC, None, ALU.mult).then_inc(nm, 1)
                    v.wait_ge(exped, n + 1)
                    link(v.reciprocal(r[:, 3:4], r[:, 2:3]))
                    v.tensor_scalar(E[:, n % 2, :], E[:, n % 2, :], r[:, 3:4], None, ALU.mult).then_inc(e_ok, 1)
                    if n:
                        v.wait_ge(op_ready, n)
                        for m in range(DK):
                            last = v.tensor_scalar(oT[:, m, (n - 1) * P:n * P], op[:, m, 0:P], bv[:, m:m + 1], None, ALU.add)
                        last.then_inc(o_ok, 1)
                v.wait_ge(op_ready, N)
                for m in range(DK):
                    last = v.tensor_scalar(oT[:, m, (N - 1) * P:N * P], op[:, m, 0:P], bv[:, m:m + 1], None, ALU.add)
                last.then_inc(o_ok, 1)

            @block.scalar
            def _(a):
                def exp(n):
                    r = row[:, n % 2, :]
                    a.wait_ge(nm, n + 1)
                    if n >= 2:
                        a.wait_ge(turned, n - 1)
                    a.activation(E[:, n % 2, :], S[:, :, :], ACT.Exp, scale=SC, bias=r[:, 1:2], accum_out=r[:, 2:3]).then_inc(exped, 1)

                exp(0)
                for n in range(N):
                    if n + 1 < N:
                        exp(n + 1)
                    a.wait_ge(turned, n + 1)
                    if n >= 2:
                        a.wait_ge(op_ready, n - 1)
                    a.activation(PT[:, n % 2], tp[:, :, :], ACT.Copy).then_inc(pt_ok, 1)


class L3Out(DenseLN):
    def __init__(self, s, K, w, o):
        super().__init__(s, K)
        self.w, self.o = w, o
        self.W = s.sb("W", [P, DK, D])
        self.b = s.sb("b", [P, KT])
        self.w_in, self.b_in = s.sem("w_in"), s.sem("b_in")

    def sync(self, e):
        e.dma_start(self.W[:, :, :], self.w["wo"]).then_inc(self.w_in, 16)
        e.dma_start(self.b[:, :], self.w["bo"]).then_inc(self.b_in, 16)

    def v_start(self, v):
        v.wait_ge(self.b_in, 16)

    def t_start(self, t):
        t.wait_ge(self.w_in, 16)

    def t_tile(self, t, i, m, acc):
        for k in range(DK):
            last = t.matmul(acc, self.W[:, k, m * P:(m + 1) * P], self.o[:, k, i * NT:(i + 1) * NT], start=k == 0, stop=k == DK - 1)
        return last

    def v_tile(self, v, i, m, acc, z, x):
        return v.scalar_tensor_tensor(z, acc, self.b[:, m:m + 1], x, ALU.add, ALU.add)


def l3_attn(nc, K, w):
    with Stage(nc, "l3") as s:
        oT = s.sb("oT", [P, DK, T])
        with Stage(nc, "l3qkv") as s1:
            qk = s1.sb("qk", [P, 2 * DK, T])
            vt = s1.sb("vt", [P, T // P, DA])
            l3_project(nc, K, w, qk, vt)
            l3_attend(nc, K, w, qk, vt, oT)
        with Stage(nc, "l3out") as s1:
            L3Out(s1, K, w, oT).run(nc)


def host_l3attn(i):
    b = i['L3_attn_bqkv']
    wo = i['L3_attn_Wo']
    return dict(wqkv=i['L3_attn_Wqkv'], bqk=b[:2 * DA].reshape(4, P).T, bv=b[2 * DA:].reshape(2, P).T,
                wo=wo.reshape(2, P, D).transpose(1, 0, 2), bo=i['L3_attn_bo'].reshape(8, P).T)



def store_state(nc, K, out):
    with nc.Block() as block:
        @block.sync
        def _(e):
            rows = out.rearrange("(k p) (b t) -> b p k t", p=P, b=BATCH)
            for b in range(BATCH):
                e.dma_start(rows[b], K.X[:, :, b, PAD:PAD + SEQ]).then_inc(K.out_stored, 16)
            e.wait_ge(K.out_stored, 16 * BATCH)


def build(nc, w, out):
    Stage.used = []
    with ExitStack() as ctx:
        K = Consts(nc, ctx)
        l0_attn(nc, K, w["l0_attn"])
        recycle(nc)
        l0_ffn(nc, K, w["l0_ffn"])
        recycle(nc)
        l1_attn(nc, K, w["l1_attn"])
        recycle(nc)
        l1_ffn(nc, K, w["l1_ffn"])
        recycle(nc)
        l2_attn(nc, K, w["l2_attn"])
        recycle(nc)
        l2_ffn(nc, K, w["l2_ffn"])
        recycle(nc)
        l3_attn(nc, K, w["l3_attn"])
        recycle(nc)
        l3_ffn(nc, K, w["l3_ffn"])
        recycle(nc)
        store_state(nc, K, out)


def kernel(**inputs):
    import concourse.bacc as bacc
    from concourse.bass_utils import run_bass_kernel_spmd

    i = {name: np.asarray(a) for name, a in inputs.items()}
    layouts = {
        "l0_attn": host_l0attn(i, i["L0_attn_x"].reshape(T, D)), "l0_ffn": host_l0ffn(i), "l1_attn": host_l1attn(i),
        "l1_ffn": host_l1ffn(i), "l2_attn": host_l2attn(i), "l2_ffn": host_l2ffn(i), "l3_attn": host_l3attn(i),
        "l3_ffn": host_l3ffn(i),
    }
    nc = bacc.Bacc("TRN2", target_bir_lowering=False, num_devices=1)
    arrays, w = {}, {}
    for layer, parts in layouts.items():
        w[layer] = {}
        for name, a in parts.items():
            a = np.ascontiguousarray(a)
            arrays[f"{layer}_{name}"] = a
            w[layer][name] = nc.dram_tensor(f"{layer}_{name}", a.shape, mybir.dt.from_np(a.dtype), kind="ExternalInput").ap()
    out = nc.dram_tensor("out_T", (D, T), F32, kind="ExternalOutput").ap()
    build(nc, w, out)
    r = run_bass_kernel_spmd(nc, [arrays], core_ids=[0])
    return np.ascontiguousarray(r.results[0]["out_T"].T).reshape(BATCH, SEQ, D)
```
